# Optimizing a Trainium2 kernel written in Bass

```python
import numpy as np
import jax
import jax.numpy as jnp

def _softmax(x, axis=-1):
    return jax.nn.softmax(x, axis=axis)

def _gelu(x):
    return jax.nn.gelu(x, approximate=True)

def _silu(x):
    return jax.nn.silu(x)

def _sigmoid(x):
    return jax.nn.sigmoid(x)

def _layernorm(x, axis=-1, eps=1e-05):
    m = jnp.mean(x, axis=axis, keepdims=True)
    v = jnp.var(x, axis=axis, keepdims=True)
    return (x - m) / jnp.sqrt(v + eps)

def _scatter_add(tgt, idx, src, axis=0):
    return tgt.at[idx].add(src)

def _segment_sum(src, seg, n):
    return jax.ops.segment_sum(src, seg, n)
kernel_name = 'mk_macaron_d1_jaxref_r8_5f1df5'

def setup_inputs(seed: int=0):
    np.random.seed(seed)
    _w = jnp.asarray

    def _L0_attn_setup():
        import jax, jax.numpy as jnp
        import numpy as np
        D_MODEL, D_INNER, D_CONV, D_STATE, DT_RANK = (128, 256, 4, 16, 64)
        ALPHA, CHUNK = (0.1, 64)

        def rmsnorm(x, w, eps=1e-05):
            return x * jax.lax.rsqrt(jnp.mean(x * x, axis=-1, keepdims=True) + eps) * w

        def mamba_block(x, in_w, in_b, conv_w, conv_b, xp_w, dt_w, dt_b, A_log, D_ssm, out_w, out_b):
            B, T, _ = x.shape
            xz = x @ in_w.T + in_b
            xm, res = jnp.split(xz, 2, axis=-1)
            xc = jax.lax.conv_general_dilated(xm.transpose(0, 2, 1), conv_w, (1,), [(D_CONV - 1, 0)], dimension_numbers=('NCH', 'OIH', 'NCH'), feature_group_count=D_INNER)
            xm = jax.nn.silu(xc.transpose(0, 2, 1) + conv_b)
            x_dbl = xm @ xp_w.T
            delta = jax.nn.softplus(x_dbl[..., :DT_RANK] @ dt_w.T + dt_b)
            Bm = x_dbl[..., DT_RANK:DT_RANK + D_STATE]
            Cm = x_dbl[..., DT_RANK + D_STATE:]
            A = -jnp.exp(A_log)

            def step(h, ins):
                d_t, B_t, C_t, u_t = ins
                dA = jnp.exp(d_t[:, :, None] * A)
                h = h * dA + (d_t * u_t)[:, :, None] * B_t[:, None, :]
                y = jnp.einsum('bds,bs->bd', h, C_t)
                return (h, y)
            h0 = jnp.zeros((B, D_INNER, D_STATE), x.dtype)
            _, ys = jax.lax.scan(step, h0, (delta.transpose(1, 0, 2), Bm.transpose(1, 0, 2), Cm.transpose(1, 0, 2), xm.transpose(1, 0, 2)))
            y = ys.transpose(1, 0, 2) + xm * D_ssm
            y = y * jax.nn.silu(res)
            return y @ out_w.T + out_b

        def memory_attend(out, w_write, w_read, decay):
            B, T, D = out.shape
            C = CHUNK
            gamma = jax.nn.sigmoid(decay)
            log_gamma = jnp.log(gamma)
            v = out @ w_write.T
            wk = jnp.pad(out[:, :-1], ((0, 0), (1, 0), (0, 0)))
            rk = out
            n = T // C
            p = jnp.arange(C)
            diffs = jnp.clip(p[:, None] - 1 - p[None, :], 0, None).astype(out.dtype)
            causal = (p[:, None] > p[None, :]).astype(out.dtype)
            M = jnp.exp(diffs * log_gamma) * causal
            g_in = gamma ** p
            g_w = gamma ** (C - 1 - p)
            chunked = lambda a: a.reshape(B, n, C, D).transpose(1, 0, 2, 3)

            def step(W, ins):
                rk_c, wk_c, v_c = ins
                inter = jnp.einsum('bde,bce->bcd', W, rk_c) * g_in[None, :, None]
                S = jnp.einsum('bcd,bkd->bck', rk_c, wk_c)
                intra = jnp.einsum('bck,bkd->bcd', S * M, v_c)
                W_new = gamma ** C * W + jnp.einsum('bcd,bce->bde', v_c * g_w[None, :, None], wk_c)
                return (W_new, inter + intra)
            W0 = jnp.zeros((B, D, D), out.dtype)
            _, reads = jax.lax.scan(step, W0, (chunked(rk), chunked(wk), chunked(v)))
            reads = reads.transpose(1, 0, 2, 3).reshape(B, T, D)
            return out + ALPHA * (reads @ w_read.T)
        key = jax.random.key(seed)
        ks = jax.random.split(key, 10)
        B, T = (2, 256)
        s = lambda k, shape, scale: jax.random.normal(k, shape, jnp.float32) * scale
        return {'x': s(ks[0], (B, T, D_MODEL), 1.0), 'norm1_w': jnp.ones((D_MODEL,), jnp.float32), 'norm2_w': jnp.ones((D_MODEL,), jnp.float32), 'in_proj_w': s(ks[1], (2 * D_INNER, D_MODEL), 0.02), 'in_proj_b': jnp.zeros((2 * D_INNER,), jnp.float32), 'conv_w': s(ks[2], (D_INNER, 1, D_CONV), 0.1), 'conv_b': jnp.zeros((D_INNER,), jnp.float32), 'x_proj_w': s(ks[3], (DT_RANK + 2 * D_STATE, D_INNER), 0.02), 'dt_proj_w': s(ks[4], (D_INNER, DT_RANK), 0.02), 'dt_proj_b': s(ks[5], (D_INNER,), 0.02), 'A_log': jnp.log(jnp.broadcast_to(jnp.arange(1, D_STATE + 1, dtype=jnp.float32), (D_INNER, D_STATE))) + 0.0, 'D_ssm': jnp.ones((D_INNER,), jnp.float32), 'out_proj_w': s(ks[6], (D_MODEL, D_INNER), 0.02), 'out_proj_b': jnp.zeros((D_MODEL,), jnp.float32), 'proj_write_w': s(ks[7], (D_MODEL, D_MODEL), 0.02), 'proj_read_w': s(ks[8], (D_MODEL, D_MODEL), 0.02), 'decay': jnp.float32(4.6)}
    _L0_attn_in = _L0_attn_setup()

    def _L0_ffn_setup():
        import jax, jax.numpy as jnp
        import numpy as np
        TOP_K = 2
        key = jax.random.key(seed)
        kx, kg, k1, k2 = jax.random.split(key, 4)
        B, T, D, E = (4, 512, 128, 8)
        H = 4 * D
        x = jax.random.normal(kx, (B, T, D), dtype=jnp.float32)
        gate_w = jax.random.normal(kg, (D, E), dtype=jnp.float32) * 0.02
        w1s = jax.random.normal(k1, (E, D, H), dtype=jnp.float32) * 0.02
        w2s = jax.random.normal(k2, (E, H, D), dtype=jnp.float32) * 0.02
        return {'x': x, 'gate_w': gate_w, 'w1s': w1s, 'w2s': w2s}
    _L0_ffn_in = _L0_ffn_setup()
    _d = {'L0_attn_x': _L0_attn_in['x'], 'L0_attn_norm1_w': _L0_attn_in['norm1_w'], 'L0_attn_norm2_w': _L0_attn_in['norm2_w'], 'L0_attn_in_proj_w': _L0_attn_in['in_proj_w'], 'L0_attn_in_proj_b': _L0_attn_in['in_proj_b'], 'L0_attn_conv_w': _L0_attn_in['conv_w'], 'L0_attn_conv_b': _L0_attn_in['conv_b'], 'L0_attn_x_proj_w': _L0_attn_in['x_proj_w'], 'L0_attn_dt_proj_w': _L0_attn_in['dt_proj_w'], 'L0_attn_dt_proj_b': _L0_attn_in['dt_proj_b'], 'L0_attn_A_log': _L0_attn_in['A_log'], 'L0_attn_D_ssm': _L0_attn_in['D_ssm'], 'L0_attn_out_proj_w': _L0_attn_in['out_proj_w'], 'L0_attn_out_proj_b': _L0_attn_in['out_proj_b'], 'L0_attn_proj_write_w': _L0_attn_in['proj_write_w'], 'L0_attn_proj_read_w': _L0_attn_in['proj_read_w'], 'L0_attn_decay': _L0_attn_in['decay'], 'L0_ffn_gate_w': _L0_ffn_in['gate_w'], 'L0_ffn_w1s': _L0_ffn_in['w1s'], 'L0_ffn_w2s': _L0_ffn_in['w2s']}
    _x0 = _d['L0_attn_x']
    _d['L0_attn_x'] = jax.random.normal(jax.random.fold_in(jax.random.key(seed), 1), (16, 256, 128), dtype=_x0.dtype)
    del _x0
    return _d

def reference(L0_attn_x, L0_attn_norm1_w, L0_attn_norm2_w, L0_attn_in_proj_w, L0_attn_in_proj_b, L0_attn_conv_w, L0_attn_conv_b, L0_attn_x_proj_w, L0_attn_dt_proj_w, L0_attn_dt_proj_b, L0_attn_A_log, L0_attn_D_ssm, L0_attn_out_proj_w, L0_attn_out_proj_b, L0_attn_proj_write_w, L0_attn_proj_read_w, L0_attn_decay, L0_ffn_gate_w, L0_ffn_w1s, L0_ffn_w2s):

    def _L0_attn_ref(x, norm1_w, norm2_w, in_proj_w, in_proj_b, conv_w, conv_b, x_proj_w, dt_proj_w, dt_proj_b, A_log, D_ssm, out_proj_w, out_proj_b, proj_write_w, proj_read_w, decay):
        import jax, jax.numpy as jnp
        import numpy as np
        D_MODEL, D_INNER, D_CONV, D_STATE, DT_RANK = (128, 256, 4, 16, 64)
        ALPHA, CHUNK = (0.1, 64)

        def rmsnorm(x, w, eps=1e-05):
            return x * jax.lax.rsqrt(jnp.mean(x * x, axis=-1, keepdims=True) + eps) * w

        def mamba_block(x, in_w, in_b, conv_w, conv_b, xp_w, dt_w, dt_b, A_log, D_ssm, out_w, out_b):
            B, T, _ = x.shape
            xz = x @ in_w.T + in_b
            xm, res = jnp.split(xz, 2, axis=-1)
            xc = jax.lax.conv_general_dilated(xm.transpose(0, 2, 1), conv_w, (1,), [(D_CONV - 1, 0)], dimension_numbers=('NCH', 'OIH', 'NCH'), feature_group_count=D_INNER)
            xm = jax.nn.silu(xc.transpose(0, 2, 1) + conv_b)
            x_dbl = xm @ xp_w.T
            delta = jax.nn.softplus(x_dbl[..., :DT_RANK] @ dt_w.T + dt_b)
            Bm = x_dbl[..., DT_RANK:DT_RANK + D_STATE]
            Cm = x_dbl[..., DT_RANK + D_STATE:]
            A = -jnp.exp(A_log)

            def step(h, ins):
                d_t, B_t, C_t, u_t = ins
                dA = jnp.exp(d_t[:, :, None] * A)
                h = h * dA + (d_t * u_t)[:, :, None] * B_t[:, None, :]
                y = jnp.einsum('bds,bs->bd', h, C_t)
                return (h, y)
            h0 = jnp.zeros((B, D_INNER, D_STATE), x.dtype)
            _, ys = jax.lax.scan(step, h0, (delta.transpose(1, 0, 2), Bm.transpose(1, 0, 2), Cm.transpose(1, 0, 2), xm.transpose(1, 0, 2)))
            y = ys.transpose(1, 0, 2) + xm * D_ssm
            y = y * jax.nn.silu(res)
            return y @ out_w.T + out_b

        def memory_attend(out, w_write, w_read, decay):
            B, T, D = out.shape
            C = CHUNK
            gamma = jax.nn.sigmoid(decay)
            log_gamma = jnp.log(gamma)
            v = out @ w_write.T
            wk = jnp.pad(out[:, :-1], ((0, 0), (1, 0), (0, 0)))
            rk = out
            n = T // C
            p = jnp.arange(C)
            diffs = jnp.clip(p[:, None] - 1 - p[None, :], 0, None).astype(out.dtype)
            causal = (p[:, None] > p[None, :]).astype(out.dtype)
            M = jnp.exp(diffs * log_gamma) * causal
            g_in = gamma ** p
            g_w = gamma ** (C - 1 - p)
            chunked = lambda a: a.reshape(B, n, C, D).transpose(1, 0, 2, 3)

            def step(W, ins):
                rk_c, wk_c, v_c = ins
                inter = jnp.einsum('bde,bce->bcd', W, rk_c) * g_in[None, :, None]
                S = jnp.einsum('bcd,bkd->bck', rk_c, wk_c)
                intra = jnp.einsum('bck,bkd->bcd', S * M, v_c)
                W_new = gamma ** C * W + jnp.einsum('bcd,bce->bde', v_c * g_w[None, :, None], wk_c)
                return (W_new, inter + intra)
            W0 = jnp.zeros((B, D, D), out.dtype)
            _, reads = jax.lax.scan(step, W0, (chunked(rk), chunked(wk), chunked(v)))
            reads = reads.transpose(1, 0, 2, 3).reshape(B, T, D)
            return out + ALPHA * (reads @ w_read.T)
        mb = lambda h: mamba_block(h, in_proj_w, in_proj_b, conv_w, conv_b, x_proj_w, dt_proj_w, dt_proj_b, A_log, D_ssm, out_proj_w, out_proj_b)
        out1 = mb(rmsnorm(x, norm1_w))
        x1 = x + out1
        out2 = mb(rmsnorm(x1, norm2_w))
        out2 = memory_attend(out2, proj_write_w, proj_read_w, decay)
        return x1 + out2

    def _L0_ffn_ref(x, gate_w, w1s, w2s):
        import jax, jax.numpy as jnp
        import numpy as np
        TOP_K = 2
        B, T, D = x.shape
        E = gate_w.shape[1]
        xf = x.reshape(-1, D)
        N = xf.shape[0]
        logits = xf @ gate_w
        probs = jax.nn.softmax(logits, axis=-1)
        vals, idx = jax.lax.top_k(probs, TOP_K)
        vals = vals / jnp.sum(vals, axis=-1, keepdims=True)
        combine = jnp.zeros((N, E), dtype=xf.dtype).at[jnp.arange(N)[:, None], idx].add(vals)
        out = jnp.zeros_like(xf)
        for e in range(E):
            h = jax.nn.silu(xf @ w1s[e])
            out = out + combine[:, e:e + 1] * (h @ w2s[e])
        return out.reshape(B, T, D)
    x = L0_attn_x
    x = x + 0.5 * _L0_ffn_ref(_layernorm(x, axis=-1), L0_ffn_gate_w, L0_ffn_w1s, L0_ffn_w2s)
    x = x + _L0_attn_ref(_layernorm(x, axis=-1), L0_attn_norm1_w, L0_attn_norm2_w, L0_attn_in_proj_w, L0_attn_in_proj_b, L0_attn_conv_w, L0_attn_conv_b, L0_attn_x_proj_w, L0_attn_dt_proj_w, L0_attn_dt_proj_b, L0_attn_A_log, L0_attn_D_ssm, L0_attn_out_proj_w, L0_attn_out_proj_b, L0_attn_proj_write_w, L0_attn_proj_read_w, L0_attn_decay)
    x = x + 0.5 * _L0_ffn_ref(_layernorm(x, axis=-1), L0_ffn_gate_w, L0_ffn_w1s, L0_ffn_w2s)
    return x

_drawn_inputs = setup_inputs


def setup_inputs(seed=0):
    import zlib

    import numpy as np

    out = dict(_drawn_inputs(seed))
    spreads = {'L0_attn_norm1_w': (1.0, 0.2),
     'L0_attn_norm2_w': (1.0, 0.2),
     'L0_attn_in_proj_b': (0.0, 0.1),
     'L0_attn_conv_b': (0.0, 0.1),
     'L0_attn_D_ssm': (1.0, 0.2),
     'L0_attn_out_proj_b': (0.0, 0.1)}
    factors = {}
    for name, (base, spread) in spreads.items():
        noise = np.random.default_rng([zlib.crc32(name.encode()), seed]).standard_normal(out[name].shape)
        drawn = base * np.exp(spread * noise) if base else spread * noise
        out[name] = jnp.asarray(drawn.astype(out[name].dtype))
    for name, factor in factors.items():
        out[name] = (out[name] * factor).astype(out[name].dtype)
    return out
```

```python
import concourse.bass as bass
from concourse import mybir
from contextlib import ExitStack

P = 128
BATCH, T, D = 16, 256, 128
E, HID = 8, 512
DI, DS, DR, DC = 256, 16, 64, 4
SEQ = 2
TOK = SEQ * T
TILES = TOK // P
GROUPS = BATCH // SEQ
HC = HID // P
HALVES = DI // P
PAD = DC - 1
EPS = 1e-5

PACK = [("in_w", 2 * DI), ("gate", E), ("xp_dt", HALVES * DR), ("xp_bc", HALVES * 4 * DS),
        ("out_w", HALVES * D), ("write_w", D), ("read_w", D), ("norm1", 1), ("norm2", 1),
        ("in_b", 2 * HALVES), ("conv_w", HALVES * DC), ("conv_b", HALVES), ("dt_b", HALVES),
        ("A_log", HALVES * DS), ("D_ssm", HALVES), ("out_b", 1), ("decay", 1), ("dt_w", DI),
        ("out_b_row", D), ("ident", P), ("dist", T), ("causal", T), ("iota", E), ("ones_row", P)]

SPREAD = [t for s in range(DS + 2) for t in ((0, s), (1, s - 2)) if 0 <= t[1] < DS]
COL, WIDTH = {}, 0
for _name, _w in PACK:
    COL[_name] = (WIDTH, WIDTH + _w)
    WIDTH += _w


def moe_mamba_kernel(nc, x, pack, sel, w1, w2, out):
    fp32, fp32r, u32 = mybir.dt.float32, mybir.dt.float32r, mybir.dt.uint32
    ALU, ACT = mybir.AluOpType, mybir.ActivationFunctionType

    ctx = ExitStack()
    with ctx:
        def sb(name, shape, dt=fp32):
            return ctx.enter_context(nc.sbuf_tensor(name, shape, dt))

        prm = sb("prm", [P, WIDTH])
        raw = sb("raw", [P, E * HID])
        w1h = sb("w1h", [P, E, HID], fp32r)
        w1l = sb("w1l", [P, E, HID], fp32r)
        w2s = sb("w2s", [P, E, HC, D])
        selr = sb("selr", [4 * DS, 2 * DS, P], fp32r)
        gh = sb("gh", [P, E], fp32r)
        gl = sb("gl", [P, E], fp32r)
        inw = sb("inw", [P, 2, 2 * DI])
        A = sb("A", [P, HALVES, DS])
        MT = sb("MT", [P, T])
        lgam = sb("lgam", [P, 4])
        powh = sb("powh", [P, TILES])
        epst = sb("epst", [P, TILES])

        def par(name):
            a, b = COL[name]
            return prm[:, a:b]

        xin = sb("xin", [P, TILES, D])
        stats = sb("stats", [P, TILES, 6])
        mv = sb("mv", [P, TILES, 2])
        rstd = sb("rstd", [P, TILES])
        xn = sb("xn", [P, TILES, D])
        xh = sb("xh", [P, TOK], fp32r)
        xl = sb("xl", [P, TOK], fp32r)
        lg = sb("lg", [P, TILES, E])
        m8 = sb("m8", [P, TILES, 8])
        ix = sb("ix", [P, TILES, 8], u32)
        ixf = sb("ixf", [P, TILES, 8])
        gap = sb("gap", [P, TILES])
        th = sb("th", [P, TILES])
        c01 = sb("c01", [P, 2, TILES])
        hit = sb("hit", [P, 2, TILES, E])
        comb = sb("comb", [P, TILES, E])
        hT = [raw[:, i * HC * TOK:(i + 1) * HC * TOK].rearrange("p (c t) -> p c t", c=HC)
              for i in range(2)]
        facc = sb("facc", [P, TILES, D])
        xa = sb("xa", [P, TILES, D])
        xb = sb("xb", [P, TILES, D])
        ob = sb("ob", [P, TILES, D])

        xam = sb("xam", [P, TILES, D])
        statm = sb("statm", [P, TILES, 6])
        mvm = sb("mvm", [P, TILES, 2])
        rstdm = sb("rstdm", [P, TILES])
        statr = sb("statr", [P, TILES, 6])
        mvr = sb("mvr", [P, TILES, 2])
        rstdr = sb("rstdr", [P, TILES])
        varr = sb("varr", [P, TILES])
        ln = sb("ln", [P, TILES, D])
        x1 = sb("x1", [P, TILES, D])
        rs = sb("rs", [P, TILES, D])
        un = sb("un", [P, TILES, D])
        uT = sb("uT", [P, TOK])
        xpad = sb("xpad", [P, HALVES, SEQ, PAD + T])
        xm = sb("xm", [P, HALVES, TOK])
        sres = sb("sres", [P, HALVES, TOK])
        dtT = sb("dtT", [DR, TOK])
        bcr = sb("bcr", [4 * DS, TOK], fp32r)
        delta = sb("delta", [P, HALVES, SEQ, T])
        du = sb("du", [P, HALVES, TOK])
        dA = [sb(f"dA{i}", [P, HALVES, SEQ, T]) for i in range(4)]
        dbu = [sb(f"dbu{i}", [P, HALVES, TOK]) for i in range(2)]
        hs = [sb(f"hs{i}", [P, HALVES, TOK]) for i in range(2)]
        G = [sb(f"G{i}", [P, HALVES, TOK]) for i in range(4)]
        gs = [sb(f"gs{i}", [P, HALVES, TOK]) for i in range(2)]
        oT = sb("oT", [P, SEQ, 1 + T])
        vt = G[0][:, 0, :].rearrange("p (j d) -> p j d", d=D)
        rT = G[0][:, 1, :]
        SM = G[1][:, :, :].rearrange("p h t -> p (h t)")[:, 0:SEQ * (T + P)].rearrange("p (b t) -> p b t", b=SEQ)
        conv, z, ez, yg = hs[0], dbu[0], dbu[1], hs[1]

        bank = [ctx.enter_context(nc.psum_tensor(n, [P, 512], fp32))
                for n in ("b_out", "b_h0", "b_h1", "b_y0", "b_y1", "b_r0", "b_r1", "b_r2")]
        OUT, H, Y, R = bank[0], bank[1:3], bank[3:5], bank[5:8]

        def sem(name):
            return ctx.enter_context(nc.semaphore(name))

        s_pack, s_w1, s_w2, s_sel = sem("s_pack"), sem("s_w1"), sem("s_w2"), sem("s_sel")
        s_raw_read, s_lg, s_Aexp, s_set_dve, s_set_act, s_exponent, s_prep = (
            sem("s_raw_read"), sem("s_lg"), sem("s_Aexp"), sem("s_set_dve"), sem("s_set_act"),
            sem("s_exponent"), sem("s_prep"))
        s_xin, s_store = sem("s_xin"), sem("s_store")
        f_stats, f_rstd, f_xn, f_xnT, f_split, f_logits, f_lread, f_gap, f_th = (
            sem("f_stats"), sem("f_rstd"), sem("f_xn"), sem("f_xnT"), sem("f_split"),
            sem("f_logits"), sem("f_lread"), sem("f_gap"), sem("f_th"))
        f_hmm, f_hact, f_ymm, f_yacc = sem("f_hmm"), sem("f_hact"), sem("f_ymm"), sem("f_yacc")
        g_stats, g_rstd, g_xam, g_ln, g_x1, g_rs, g_xb = (
            sem("g_stats"), sem("g_rstd"), sem("g_xam"), sem("g_ln"), sem("g_x1"), sem("g_rs"), sem("g_xb"))
        g_oTmm, g_oT, g_vmm, g_v, g_smm, g_sm, g_rmm, g_r = (
            sem("g_oTmm"), sem("g_oT"), sem("g_vmm"), sem("g_v"), sem("g_smm"), sem("g_sm"),
            sem("g_rmm"), sem("g_r"))
        q_stats, q_rstd, q_u, q_uTmm, q_uT, q_xz, q_xpad, q_conv, q_xm, q_res = (
            sem("q_stats"), sem("q_rstd"), sem("q_u"), sem("q_uTmm"), sem("q_uT"), sem("q_xz"),
            sem("q_xpad"), sem("q_conv"), sem("q_xm"), sem("q_res"))
        q_bcmm, q_bc, q_dtmm, q_dt, q_zmm, q_sp, q_delta = (
            sem("q_bcmm"), sem("q_bc"), sem("q_dtmm"), sem("q_dt"), sem("q_zmm"), sem("q_sp"), sem("q_delta"))
        q_dA, q_B, q_C, q_dbu, q_scan, q_G, q_gs, q_ymm, q_yg, q_omm = (
            sem("q_dA"), sem("q_B"), sem("q_C"), sem("q_dbu"), sem("q_scan"), sem("q_G"),
            sem("q_gs"), sem("q_ymm"), sem("q_yg"), sem("q_omm"))

        def wait(eng, s, value):
            if not isinstance(value, int) or value > 0:
                eng.wait_ge(s, value)

        block = ctx.enter_context(nc.Block())

        @block.sync
        def _(sp):
            xt = x.rearrange("(g j p) d -> g p j d", p=P, j=TILES)
            ot = out.rearrange("(g j p) d -> g p j d", p=P, j=TILES)
            sp.dma_start(prm[:, :], pack).then_inc(s_pack, 16)
            sp.dma_start(xin[:, :, :], xt[0]).then_inc(s_xin, 16)
            sp.dma_start(raw[:, :].rearrange("p (e h) -> p e h", e=E),
                         w1.rearrange("e d h -> d e h")).then_inc(s_w1, 16)
            sp.dma_start(w2s[:, :, :, :].rearrange("p e c d -> p (e c) d"),
                         w2.rearrange("e (c p) d -> p (e c) d", p=P)).then_inc(s_w2, 16)
            sp.wait_ge(s_raw_read, 1)
            sp.dma_start(raw[0:4 * DS, :], sel).then_inc(s_sel, 16)
            for g in range(GROUPS):
                if g + 1 < GROUPS:
                    sp.wait_ge(f_yacc, 2 * g * E + 1)
                    sp.dma_start(xin[:, :, :], xt[g + 1]).then_inc(s_xin, 16)
                sp.wait_ge(f_yacc, (2 * g + 2) * E)
                sp.dma_start(ot[g], ob[:, :, :]).then_inc(s_store, 16)
            sp.wait_ge(s_store, 16 * GROUPS)

        @block.tensor
        def _(pe):
            mm = nc.tensor.matmul
            ident = par("ident")

            def ffn_pre(n):
                pe.wait_ge(f_xn, n + 1)
                wait(pe, f_yacc, n * E)
                for j in range(TILES):
                    last = nc.tensor.transpose(OUT[:, j * P:(j + 1) * P], xn[:, j, :], ident)
                last.then_inc(f_xnT, 1)
                pe.wait_ge(f_split, n + 1)
                wait(pe, f_hact, n * E * HC)
                for j in range(TILES):
                    t = slice(j * P, (j + 1) * P)
                    for k, (a, b) in enumerate(((xh, gh), (xh, gl), (xl, gh), (xl, gl))):
                        last = mm(H[0][:, j * E:(j + 1) * E], a[:, t], b[:, :], start=k == 0, stop=k == 3)
                last.then_inc(f_logits, 1)

            def ffn_up(n, e, c):
                i = e * HC + c
                if i == 0:
                    pe.wait_ge(f_lread, n + 1)
                else:
                    wait(pe, f_hact, n * E * HC + i - 1)
                w = slice(c * P, (c + 1) * P)
                h = H[i % 2][:, :]
                mm(h, w1h[:, e, w], xh[:, :], start=True, stop=False)
                mm(h, w1h[:, e, w], xl[:, :], start=False, stop=False)
                mm(h, w1l[:, e, w], xh[:, :], start=False, stop=True).then_inc(f_hmm, 1)

            def ffn_down(n, e, j):
                if j == 0:
                    pe.wait_ge(f_hact, (n * E + e + 1) * HC)
                    wait(pe, f_yacc, n * E + e)
                for c in range(HC):
                    last = mm(OUT[:, j * D:(j + 1) * D], hT[e % 2][:, c, j * P:(j + 1) * P], w2s[:, e, c, :],
                              start=c == 0, stop=c == HC - 1)
                if j == TILES - 1:
                    last.then_inc(f_ymm, 1)

            def ffn(n):
                ffn_pre(n)
                for c in range(HC):
                    ffn_up(n, 0, c)
                for e in range(E):
                    if e + 1 < E:
                        for c in range(HC):
                            ffn_up(n, e + 1, c)
                    for j in range(TILES):
                        ffn_down(n, e, j)

            def mamba_head(g, m):
                q = g * 2 + m
                pe.wait_ge(q_u, q + 1)
                for j in range(TILES):
                    last = nc.tensor.transpose(R[0][:, j * P:(j + 1) * P], un[:, j, :], ident)
                last.then_inc(q_uTmm, 1)
                pe.wait_ge(q_uT, q + 1)
                wait(pe, q_yg, q)
                if m == 0:
                    wait(pe, g_sm, 2 * g)
                    wait(pe, g_v, g)
                    wait(pe, g_r, g)
                for k, b in enumerate((Y[0], Y[1], R[1], R[2])):
                    mm(b[:, :], inw[:, m, k * P:(k + 1) * P], uT[:, :], start=True, stop=True).then_inc(q_xz, 1)
                pe.wait_ge(q_xm, 2 * q + 2)
                wt, wb = par("xp_dt"), par("xp_bc")
                for k in range(HALVES):
                    last = mm(R[0][0:DR, :], wt[:, k * DR:(k + 1) * DR], xm[:, k, :],
                              start=k == 0, stop=k == HALVES - 1)
                last.then_inc(q_dtmm, 1)
                for k in range(HALVES):
                    last = mm(Y[0][0:4 * DS, :], wb[:, k * 4 * DS:(k + 1) * 4 * DS], xm[:, k, :],
                              start=k == 0, stop=k == HALVES - 1)
                last.then_inc(q_bcmm, 1)
                pe.wait_ge(q_dt, q + 1)
                for k in range(HALVES):
                    mm(R[1 + k][:, :], par("dt_w")[0:DR, k * P:(k + 1) * P], dtT[:, :],
                       start=True, stop=True).then_inc(q_zmm, 1)

            def spread(g, m, i):
                q = g * 2 + m
                if i == 0:
                    pe.wait_ge(q_bc, q + 1)
                if i < 3:
                    pe.wait_ge(q_sp, q + 1)
                else:
                    kind, s = SPREAD[i - 3]
                    pe.wait_ge(q_G if kind else q_dbu, q * DS + s + 1)
                kind, s = SPREAD[i]
                mm(R[i % 3][:, :], selr[:, kind * DS + s, :], bcr[:, :], start=True, stop=True)\
                    .then_inc(q_C if kind else q_B, 1)

            def reduce(g, m, p):
                q = g * 2 + m
                pe.wait_ge(q_gs, q * (DS // 2) + p + 1)
                for k in range(HALVES):
                    last = mm(Y[k][:, :], ident, gs[p % 2][:, k, :], start=p == 0, stop=p == DS // 2 - 1)
                last.then_inc(q_ymm, 1)

            def scan(g, m):
                for i in range(2 * DS):
                    spread(g, m, i)
                    if i % 4 == 3 and i >= 11:
                        reduce(g, m, (i - 11) // 4)
                reduce(g, m, DS // 2 - 2)
                reduce(g, m, DS // 2 - 1)

            def out_proj(g, m):
                q = g * 2 + m
                pe.wait_ge(q_yg, q + 1)
                for j in range(TILES):
                    for k in range(HALVES):
                        mm(R[0][:, j * D:(j + 1) * D], yg[:, k, j * P:(j + 1) * P],
                           par("out_w")[:, k * D:(k + 1) * D], start=j == k == 0, stop=False,
                           skip_group_check=True)
                if m == 0:
                    add_bias()

            def add_bias():
                mm(R[0][:, :], par("ones_row"), par("out_b_row").unsqueeze(1).broadcast_to([P, TILES, D]),
                   start=False, stop=True, skip_group_check=True).then_inc(q_omm, 1)

            def memory(g):
                q = g * 2 + 1
                for k in range(HALVES):
                    last = mm(R[1][:, :], par("out_w")[:, k * D:(k + 1) * D], yg[:, k, :],
                              start=k == 0, stop=k == HALVES - 1)
                last.then_inc(g_oTmm, 1)
                pe.wait_ge(g_oT, g + 1)
                for j in range(TILES):
                    b, t = j // 2, (j % 2) * P
                    last = mm(R[2][:, j * D:(j + 1) * D], oT[:, b, 1 + t:1 + t + P], par("write_w"),
                              start=True, stop=True)
                last.then_inc(g_vmm, 1)
                for b in range(SEQ):
                    mm(Y[b][:, 0:T], oT[:, b, 0:P], oT[:, b, 1:1 + T], start=True, stop=True)
                    mm(Y[b][:, T:T + P], oT[:, b, P:T], oT[:, b, 1 + P:1 + T], start=True, stop=True)\
                        .then_inc(g_smm, 1)
                pe.wait_ge(g_v, g + 1)
                for b in range(SEQ):
                    pe.wait_ge(g_sm, 2 * g + b + 1)
                    first, second = (R[1][:, b * T + t:b * T + t + P] for t in (0, P))
                    mm(first, vt[:, 2 * b, :], SM[:, b, 0:P], start=True, stop=True)
                    mm(second, vt[:, 2 * b, :], SM[:, b, P:T], start=True, stop=False)
                    last = mm(second, vt[:, 2 * b + 1, :], SM[:, b, T:T + P], start=False, stop=True)
                last.then_inc(g_rmm, 1)
                pe.wait_ge(g_r, g + 1)
                for j in range(TILES):
                    mm(R[0][:, j * D:(j + 1) * D], rT[:, j * P:(j + 1) * P], par("read_w"),
                       start=False, stop=False, skip_group_check=True)
                add_bias()

            pe.wait_ge(s_pack, 16)
            pe.wait_ge(s_w2, 16)
            pe.wait_ge(s_set_dve, 1)
            def group(g):
                ffn(g * 2)
                for m in range(2):
                    mamba_head(g, m)
                    scan(g, m)
                    out_proj(g, m)
                memory(g)
                ffn(g * 2 + 1)

            group(0)
            with pe.Fori(1, GROUPS) as g:
                group(g)

        @block.scalar
        def _(act):
            do = nc.scalar.activation

            act.wait_ge(s_pack, 16)
            do(lgam[:, 0:1], par("decay"), ACT.Abs)
            act.drain()
            do(lgam[:, 1:2], lgam[:, 0:1], ACT.Exp, scale=-1.0)
            act.drain()
            do(lgam[:, 2:3], lgam[:, 1:2], ACT.Ln, bias=1.0).then_inc(s_lg, 1)
            do(A[:, :, :], par("A_log").rearrange("p (h s) -> p h s", s=DS), ACT.Exp).then_inc(s_Aexp, 1)
            act.wait_ge(s_exponent, 1)
            do(MT[:, :], par("dist"), ACT.Exp, scale=lgam[:, 3:4]).then_inc(s_set_act, 1)
            act.wait_ge(s_set_dve, 1)

            def ffn_gate(n):
                act.wait_ge(f_gap, n + 1)
                do(th[:, :], gap[:, :], ACT.Tanh, scale=0.5).then_inc(f_th, 1)

            def ffn_silu(n, e, c):
                i = e * HC + c
                if c == 0:
                    wait(act, f_ymm, n * E + e - 1)
                act.wait_ge(f_hmm, n * E * HC + i + 1)
                do(hT[e % 2][:, c, :], H[i % 2][:, :], ACT.Silu).then_inc(f_hact, 1)

            def ffn(n):
                ffn_gate(n)
                for e in range(E):
                    for c in range(HC):
                        ffn_silu(n, e, c)

            def mamba_head(g, m):
                q = g * 2 + m
                act.wait_ge(q_uTmm, q + 1)
                do(uT[:, :], R[0][:, :], ACT.Copy).then_inc(q_uT, 1)
                for k in range(HALVES):
                    act.wait_ge(q_xz, 4 * q + k + 1)
                    do(xpad[:, k, :, PAD:], Y[k][:, :].rearrange("p (b t) -> p b t", b=SEQ), ACT.Identity,
                       bias=par("in_b")[:, k:k + 1]).then_inc(q_xpad, 1)
                for k in range(HALVES):
                    act.wait_ge(q_xz, 4 * q + 3 + k)
                    do(sres[:, k, :], R[1 + k][:, :], ACT.Silu, bias=par("in_b")[:, 2 + k:3 + k]).then_inc(q_res, 1)
                for k in range(HALVES):
                    act.wait_ge(q_conv, 2 * q + k + 1)
                    do(xm[:, k, :], conv[:, k, :], ACT.Silu, bias=par("conv_b")[:, k:k + 1]).then_inc(q_xm, 1)
                act.wait_ge(q_dtmm, q + 1)
                do(dtT[:, :], R[0][0:DR, :], ACT.Copy).then_inc(q_dt, 1)
                for k in range(HALVES):
                    act.wait_ge(q_zmm, 2 * q + k + 1)
                    do(z[:, k, :], R[1 + k][:, :], ACT.Identity, bias=par("dt_b")[:, k:k + 1])
                act.drain()
                do(ez[:, :, :], z[:, :, :], ACT.Abs)
                act.drain()
                do(ez[:, :, :], ez[:, :, :], ACT.Exp, scale=-1.0)
                act.drain()
                do(ez[:, :, :], ez[:, :, :], ACT.Ln, bias=1.0).then_inc(q_sp, 1)

            def decay_step(g, m, s):
                q = g * 2 + m
                if s == 0:
                    act.wait_ge(q_delta, q + 1)
                wait(act, q_scan, q * DS + s - 3)
                for k in range(HALVES):
                    last = do(dA[s % 4][:, k, :, 1:], delta[:, k, :, 1:], ACT.Exp, scale=A[:, k, s:s + 1])
                last.then_inc(q_dA, 1)

            def memory(g):
                act.wait_ge(g_oTmm, g + 1)
                do(oT[:, :, 1:], R[1][:, :].rearrange("p (b t) -> p b t", b=SEQ), ACT.Identity,
                   bias=par("out_b")).then_inc(g_oT, 1)
                act.wait_ge(g_vmm, g + 1)
                do(vt[:, :, :], R[2][:, :].rearrange("p (j d) -> p j d", d=D), ACT.Copy).then_inc(g_v, 1)
                act.wait_ge(g_rmm, g + 1)
                do(rT[:, :], R[1][:, :], ACT.Copy).then_inc(g_r, 1)

            def group(g):
                ffn(g * 2)
                for m in range(2):
                    mamba_head(g, m)
                    for s in range(DS):
                        decay_step(g, m, s)
                memory(g)
                ffn(g * 2 + 1)

            group(0)
            with act.Fori(1, GROUPS) as g:
                group(g)

        @block.vector
        def _(dve):
            V = nc.vector

            def norm_stats(src, st, agg):
                for j in range(TILES):
                    V.bn_stats(st[:, j, :], src[:, j, :])
                dve.drain()
                for j in range(TILES):
                    last = V.bn_aggr(agg[:, j, :], st[:, j, :])
                return last

            V.memset(oT[:, :, 0:1], 0.0)
            V.memset(xpad[:, :, :, 0:PAD], 0.0)
            for i in range(4):
                V.memset(dA[i][:, :, :, 0:1], 0.0)
            dve.wait_ge(s_pack, 16)
            for m, nw in enumerate(("norm1", "norm2")):
                V.tensor_scalar(inw[:, m, :], par("in_w"), par(nw), None, ALU.mult)
            V.tensor_copy(gh[:, :], par("gate"))
            V.tensor_scalar(par("read_w"), par("read_w"), 0.1, None, ALU.mult)
            dve.drain()
            V.tensor_tensor(gl[:, :], par("gate"), gh[:, :].bitcast(fp32), ALU.subtract)
            dve.wait_ge(s_lg, 1)
            V.tensor_scalar(lgam[:, 0:1], par("decay"), 0.0, None, ALU.min)
            dve.drain()
            V.tensor_tensor(lgam[:, 3:4], lgam[:, 0:1], lgam[:, 2:3], ALU.subtract).then_inc(s_exponent, 1)
            dve.wait_ge(s_w1, 16)
            rv = raw[:, :].rearrange("p (e h) -> p e h", e=E)
            V.tensor_copy(w1h[:, :, :], rv)
            dve.drain()
            V.tensor_tensor(w1l[:, :, :], rv, w1h[:, :, :].bitcast(fp32), ALU.subtract).then_inc(s_raw_read, 1)
            dve.wait_ge(s_Aexp, 1)
            V.tensor_scalar(A[:, :, :], A[:, :, :], -1.0, None, ALU.mult)
            dve.wait_ge(s_set_act, 1)
            V.tensor_tensor(MT[:, :], MT[:, :], par("causal"), ALU.mult)
            dve.wait_ge(s_sel, 16)
            V.tensor_copy(selr[:, :, :], raw[0:4 * DS, :].rearrange("p (i m) -> p i m", m=P))
            dve.drain()
            V.memset(gap[:, :], 0.0).then_inc(s_set_dve, 1)

            def ffn_pre(n, src):
                norm_stats(src, stats, mv).then_inc(f_stats, 1)
                dve.wait_ge(f_rstd, n + 1)
                wait(dve, f_xnT, n)
                for j in range(TILES):
                    last = V.tensor_scalar(xn[:, j, :], src[:, j, :], mv[:, j, 0:1], rstd[:, j:j + 1],
                                           ALU.subtract, ALU.mult)
                last.then_inc(f_xn, 1)
                dve.wait_ge(f_xnT, n + 1)
                wait(dve, f_hmm, n * E * HC)
                V.tensor_copy(xh[:, :], OUT[:, :])
                dve.drain()
                V.tensor_tensor(xl[:, :], OUT[:, :], xh[:, :].bitcast(fp32), ALU.subtract).then_inc(f_split, 1)
                dve.wait_ge(f_logits, n + 1)
                V.tensor_copy(lg[:, :, :], H[0][:, 0:TILES * E].rearrange("p (j e) -> p j e", e=E))\
                    .then_inc(f_lread, 1)
                dve.drain()
                for j in range(TILES):
                    V.max(m8[:, j, :], lg[:, j, :])
                dve.drain()
                V.tensor_tensor(gap[:, :], m8[:, :, 0], m8[:, :, 1], ALU.subtract).then_inc(f_gap, 1)
                for j in range(TILES):
                    V.max_index(ix[:, j, :], m8[:, j, :], lg[:, j, :])
                dve.drain()
                V.tensor_copy(ixf[:, :, :], ix[:, :, :])
                dve.wait_ge(f_th, n + 1)
                V.tensor_scalar(c01[:, 0, :], th[:, :], 0.25, 0.25, ALU.mult, ALU.add)
                V.tensor_scalar(c01[:, 1, :], th[:, :], -0.25, 0.25, ALU.mult, ALU.add)
                dve.drain()
                iota = par("iota").unsqueeze(1).broadcast_to([P, TILES, E])
                for k in range(2):
                    V.tensor_tensor(hit[:, k, :, :], iota, ixf[:, :, k:k + 1].broadcast_to([P, TILES, E]),
                                    ALU.is_equal)
                dve.drain()
                for k in range(2):
                    V.tensor_tensor(hit[:, k, :, :], hit[:, k, :, :],
                                    c01[:, k, :].unsqueeze(2).broadcast_to([P, TILES, E]), ALU.mult)
                dve.drain()
                V.tensor_tensor(comb[:, :, :], hit[:, 0, :, :], hit[:, 1, :, :], ALU.add)
                dve.drain()

            def ffn_sum(n, e, src, dst):
                dve.wait_ge(f_ymm, n * E + e + 1)
                wait(dve, f_yacc, n * E + e)
                for j in range(TILES):
                    last = V.scalar_tensor_tensor(
                        out=(facc if e < E - 1 else dst)[:, j, :], in0=OUT[:, j * D:(j + 1) * D],
                        scalar=comb[:, j, e:e + 1], in1=(src if e == 0 else facc)[:, j, :],
                        op0=ALU.mult, op1=ALU.add)
                last.then_inc(f_yacc, 1)

            def ffn1(g):
                dve.wait_ge(s_xin, g * 16 + 16)
                ffn_pre(g * 2, xin)
                for e in range(E):
                    if e == E - 1:
                        wait(dve, g_xam, g)
                    ffn_sum(g * 2, e, xin, xa)

            def ffn2(g):
                dve.wait_ge(g_xb, g + 1)
                ffn_pre(g * 2 + 1, xb)
                for e in range(E):
                    if e == E - 1:
                        wait(dve, s_store, g * 16)
                    ffn_sum(g * 2 + 1, e, xb, ob)

            def mixer_norm(g, n1):
                dve.wait_ge(f_yacc, n1 * E + E)
                norm_stats(xa, statm, mvm).then_inc(g_stats, 1)
                dve.wait_ge(g_rstd, g + 1)
                for j in range(TILES):
                    last = V.tensor_scalar(ln[:, j, :], xa[:, j, :], mvm[:, j, 0:1], rstdm[:, j:j + 1],
                                           ALU.subtract, ALU.mult)
                last.then_inc(g_ln, 1)

            def mamba_head(g, m):
                q = g * 2 + m
                src = (ln, x1)[m]
                dve.wait_ge((g_ln, g_x1)[m], g + 1)
                norm_stats(src, statr, mvr).then_inc(q_stats, 1)
                dve.wait_ge(q_rstd, q + 1)
                wait(dve, q_uTmm, q)
                for j in range(TILES):
                    last = V.tensor_scalar(un[:, j, :], src[:, j, :], rstdr[:, j:j + 1], None, ALU.mult)
                last.then_inc(q_u, 1)
                cw = par("conv_w")
                for k in range(HALVES):
                    dve.wait_ge(q_xpad, 2 * q + k + 1)
                    if k == 0:
                        wait(dve, q_omm, q)
                    cv = conv[:, k, :].rearrange("p (b t) -> p b t", b=SEQ)
                    V.tensor_scalar(cv, xpad[:, k, :, PAD:], cw[:, k * DC + PAD:k * DC + DC], None, ALU.mult)
                    for j in range(PAD):
                        dve.drain()
                        last = V.scalar_tensor_tensor(out=cv, in0=xpad[:, k, :, j:j + T],
                                                      scalar=cw[:, k * DC + j:k * DC + j + 1], in1=cv,
                                                      op0=ALU.mult, op1=ALU.add)
                    last.then_inc(q_conv, 1)
                dve.wait_ge(q_bcmm, q + 1)
                wait(dve, q_C, q * DS)
                V.tensor_copy(bcr[:, :], Y[0][0:4 * DS, :])
                dve.drain()
                lo = slice(2 * DS, 4 * DS)
                V.tensor_tensor(bcr[lo, :], Y[0][lo, :], bcr[lo, :].bitcast(fp32), ALU.subtract).then_inc(q_bc, 1)
                dve.wait_ge(q_sp, q + 1)
                V.scalar_tensor_tensor(out=delta[:, :, :, :].rearrange("p h b t -> p (h b t)"),
                                       in0=z[:, :, :].rearrange("p h t -> p (h t)"), scalar=0.0,
                                       in1=ez[:, :, :].rearrange("p h t -> p (h t)"),
                                       op0=ALU.max, op1=ALU.add).then_inc(q_delta, 1)
                dve.wait_ge(q_delta, q + 1)
                V.tensor_tensor(du[:, :, :], delta[:, :, :, :].rearrange("p h b t -> p h (b t)"), xm[:, :, :],
                                ALU.mult)
                dve.drain()

            def over_halves(b):
                return b[:, :].unsqueeze(1).broadcast_to([P, HALVES, TOK])

            def flat(b):
                return b.rearrange("p h t -> p (h t)")

            def scan(g, m):
                q = g * 2 + m
                for s in range(DS + 2):
                    if s < DS:
                        dve.wait_ge(q_B, q * DS + s + 1)
                        wait(dve, q_scan, q * DS + s - 1)
                        V.tensor_tensor(dbu[s % 2][:, :, :], du[:, :, :], over_halves(R[SPREAD.index((0, s)) % 3]), ALU.mult)\
                            .then_inc(q_dbu, 1)
                    r = s - 1
                    if 0 <= r < DS:
                        dve.wait_ge(q_dA, q * DS + r + 1)
                        dve.wait_ge(q_dbu, q * DS + r + 1)
                        wait(dve, q_G, q * DS + r - 1)
                        V.tensor_tensor_scan(flat(hs[r % 2][:, :, :]),
                                             dA[r % 4][:, :, :, :].rearrange("p h b t -> p (h b t)"),
                                             flat(dbu[r % 2][:, :, :]), 0.0, ALU.mult, ALU.add).then_inc(q_scan, 1)
                    r = s - 2
                    if r >= 0:
                        dve.wait_ge(q_C, q * DS + r + 1)
                        dve.wait_ge(q_scan, q * DS + r + 1)
                        wait(dve, q_gs, q * (DS // 2) + r // 2 - 1)
                        V.tensor_tensor(G[r % 4][:, :, :], hs[r % 2][:, :, :], over_halves(R[SPREAD.index((1, r)) % 3]),
                                        ALU.mult).then_inc(q_G, 1)

            def gate_y(g, m):
                q = g * 2 + m
                dve.wait_ge(q_ymm, (q + 1) * (DS // 2))
                dve.wait_ge(q_res, 2 * q + 2)
                for k in range(HALVES):
                    V.scalar_tensor_tensor(out=yg[:, k, :], in0=xm[:, k, :], scalar=par("D_ssm")[:, k:k + 1],
                                           in1=Y[k][:, :], op0=ALU.mult, op1=ALU.add)
                dve.drain()
                V.tensor_tensor(yg[:, :, :], yg[:, :, :], sres[:, :, :], ALU.mult).then_inc(q_yg, 1)

            def r0():
                return R[0][:, :].rearrange("p (j d) -> p j d", d=D)

            def mixer_mid(g):
                dve.wait_ge(q_omm, g * 2 + 1)
                wait(dve, g_rs, g)
                V.tensor_tensor(x1[:, :, :], r0(), ln[:, :, :], ALU.add).then_inc(g_x1, 1)

            def memory(g):
                for b in range(SEQ):
                    dve.wait_ge(g_smm, 2 * g + b + 1)
                    V.tensor_tensor(SM[:, b, 0:T], Y[b][:, 0:T], MT[:, :], ALU.mult)
                    V.tensor_tensor(SM[:, b, T:T + P], Y[b][:, T:T + P], MT[:, 0:P], ALU.mult).then_inc(g_sm, 1)
                dve.wait_ge(q_omm, g * 2 + 2)
                dve.wait_ge(g_rs, g + 1)
                V.tensor_tensor(xb[:, :, :], r0(), rs[:, :, :], ALU.add).then_inc(g_xb, 1)

            def group(g):
                ffn1(g)
                mixer_norm(g, g * 2)
                for m in range(2):
                    mamba_head(g, m)
                    scan(g, m)
                    gate_y(g, m)
                    if m == 0:
                        mixer_mid(g)
                memory(g)
                ffn2(g)

            group(0)
            with dve.Fori(1, GROUPS) as g:
                group(g)

        @block.gpsimd
        def _(pool):
            Q = nc.gpsimd
            Q.memset(powh[:, :], -0.5)
            Q.memset(epst[:, :], EPS)
            pool.drain()

            def root(v, r):
                Q.tensor_tensor(r[:, :], v, epst[:, :], ALU.add)
                pool.drain()
                return Q.tensor_tensor(r[:, :], r[:, :], powh[:, :], ALU.pow)

            def ffn_root(n):
                pool.wait_ge(f_stats, n + 1)
                root(mv[:, :, 1], rstd).then_inc(f_rstd, 1)

            def mixer_root(g):
                pool.wait_ge(g_stats, g + 1)
                root(mvm[:, :, 1], rstdm).then_inc(g_rstd, 1)
                Q.tensor_scalar(xam[:, :, :], xa[:, :, :], 1.0, 0.0, ALU.mult, ALU.add).then_inc(g_xam, 1)

            def mamba_root(g, m):
                q = g * 2 + m
                pool.wait_ge(q_stats, q + 1)
                Q.tensor_tensor(varr[:, :], mvr[:, :, 0], mvr[:, :, 0], ALU.mult)
                pool.drain()
                Q.tensor_tensor(varr[:, :], varr[:, :], mvr[:, :, 1], ALU.add)
                pool.drain()
                root(varr[:, :], rstdr).then_inc(q_rstd, 1)

            def pair_sum(g, m, p):
                q = g * 2 + m
                pool.wait_ge(q_G, q * DS + 2 * p + 2)
                wait(pool, q_ymm, q * (DS // 2) + p - 1)
                Q.tensor_tensor(gs[p % 2][:, :, :], G[(2 * p) % 4][:, :, :], G[(2 * p + 1) % 4][:, :, :],
                                ALU.add).then_inc(q_gs, 1)

            def group(g):
                ffn_root(g * 2)
                mixer_root(g)
                for m in range(2):
                    mamba_root(g, m)
                    if m == 1:
                        pool.wait_ge(g_x1, g + 1)
                        wait(pool, g_xb, g)
                        Q.tensor_tensor(rs[:, :, :], xam[:, :, :], x1[:, :, :], ALU.add).then_inc(g_rs, 1)
                    for p in range(DS // 2):
                        pair_sum(g, m, p)
                ffn_root(g * 2 + 1)

            group(0)
            with pool.Fori(1, GROUPS) as g:
                group(g)


def kernel(**inputs):
    import numpy as np
    import concourse.bacc as bacc
    from concourse.bass_utils import run_bass_kernel_spmd

    def a(name):
        return np.asarray(inputs["L0_" + name])

    def rows(m):
        return m.reshape(-1, P, m.shape[1]).transpose(1, 0, 2).reshape(P, -1)

    def fill(m, r=P):
        return np.concatenate([m, np.zeros((r - m.shape[0], m.shape[1]), m.dtype)], 0)

    t, s = np.arange(T)[None, :], np.arange(P)[:, None]
    xp = a("attn_x_proj_w")
    bc = np.concatenate([xp[DR:]] * 2, 0).T
    ob = a("attn_out_proj_b")
    f = np.float32
    parts = {
        "in_w": a("attn_in_proj_w").T, "gate": a("ffn_gate_w"),
        "xp_dt": rows(xp[:DR].T), "xp_bc": rows(bc), "out_w": rows(a("attn_out_proj_w").T),
        "write_w": a("attn_proj_write_w").T, "read_w": a("attn_proj_read_w").T,
        "norm1": a("attn_norm1_w")[:, None], "norm2": a("attn_norm2_w")[:, None],
        "in_b": rows(a("attn_in_proj_b")[:, None]), "conv_w": rows(a("attn_conv_w")[:, 0, :]),
        "conv_b": rows(a("attn_conv_b")[:, None]), "dt_b": rows(a("attn_dt_proj_b")[:, None]),
        "A_log": rows(a("attn_A_log")), "D_ssm": rows(a("attn_D_ssm")[:, None]), "out_b": ob[:, None],
        "decay": np.broadcast_to(a("attn_decay").reshape(1, 1), (P, 1)),
        "dt_w": fill(a("attn_dt_proj_w").T), "out_b_row": fill(ob[None, :]),
        "ident": np.eye(P, dtype=f), "dist": np.maximum(t - 1 - s, 0).astype(f), "causal": (t > s).astype(f),
        "iota": np.broadcast_to(np.arange(E, dtype=f), (P, E)), "ones_row": fill(np.ones((1, P), f)),
    }
    pack = np.ascontiguousarray(np.concatenate([parts[n] for n, _ in PACK], 1))
    sel = np.zeros((4 * DS, 2 * DS, P), f)
    sel[np.arange(4 * DS), np.arange(4 * DS) % (2 * DS), :] = 1.0
    arrays = {
        "x_dram": np.ascontiguousarray(a("attn_x").reshape(BATCH * T, D)), "pack_dram": pack,
        "sel_dram": sel.reshape(4 * DS, -1), "w1_dram": np.ascontiguousarray(a("ffn_w1s")),
        "w2_dram": np.ascontiguousarray(a("ffn_w2s")),
    }
    nc = bacc.Bacc("TRN2", target_bir_lowering=False, num_devices=1)
    args = [nc.dram_tensor(n, v.shape, mybir.dt.float32, kind="ExternalInput").ap() for n, v in arrays.items()]
    out = nc.dram_tensor("out_dram", (BATCH * T, D), mybir.dt.float32, kind="ExternalOutput").ap()
    moe_mamba_kernel(nc, *args, out)
    r = run_bass_kernel_spmd(nc, [arrays], core_ids=[0])
    return r.results[0]["out_dram"].reshape(BATCH, T, D)
```

```python
import concourse.bass as bass
from concourse import mybir
from contextlib import ExitStack

P = 128
BATCH, T, D = 16, 256, 128
E, HID = 8, 512
DI, DS, DR, DC = 256, 16, 64, 4
SEQ = 2
TOK = SEQ * T
TILES = TOK // P
GROUPS = BATCH // SEQ
HC = HID // P
HALVES = DI // P
PAD = DC - 1
EPS = 1e-5

PACK = [("in_w", 2 * DI), ("gate", E), ("xp_dt", HALVES * DR), ("xp_bc", HALVES * 4 * DS),
        ("out_w", HALVES * D), ("write_w", D), ("read_w", D), ("norm1", 1), ("norm2", 1),
        ("in_b", 2 * HALVES), ("conv_w", HALVES * DC), ("conv_b", HALVES), ("dt_b", HALVES),
        ("A_log", HALVES * DS), ("D_ssm", HALVES), ("out_b", 1), ("decay", 1), ("dt_w", DI),
        ("out_b_row", D), ("ident", P), ("dist", T), ("causal", T), ("iota", E), ("ones_row", P)]

DP = 2
NP = DS // DP
SPREAD = [t for j in range(NP + 1) for t in ((0, j), (1, j - 1)) if 0 <= t[1] < NP]
NG = 3
RING = 3
SHIFT = (0, 1, 2, 0)
PAIR = 4 * HC
PIECES = E // 2 * PAIR

ORDER = {
    "tensor": (
        "fturn t0 in fgate t1 t2 p4 t3 t4 p1 t5 p6 t6 t7 p1 xp t8 p1 dt p2 m1 p1 t9 p1 t10 p3 t11 t12 p2 m2 "
        "p2 t13 p1 t14 m3 p4 t15 m4 p4",
        "t0 t1 t2 p3 out p5 t3 t4 p1 turn t5 p2 in p2 t6 t7 p5 t8 p1 t9 xp p1 t10 t11 p4 t12 t13 p3 t14 p1 "
        "dt p1 t15 p2",
        "t0 t1 fturn fgate t2 p1 out p2 t3 t4 p4 t5 p1 t6 turn p1 in p3 t7 p3 t8 t9 t10 p2 xp t11 p5 t12 p3 "
        "t13 t14 p1 dt p1 t15 p1",
        "p2 t0 turng p2 in p1 t1 p1 t2 p2 t3 p8 t4 t5 xp p4 t6 dt p1 t7 t8 t9 m1 p1 t10 m2 p4 t11 t12 p3 "
        "t13 p5 t14 p1 t15 p1 m3 m4"),
    "scalar": (
        "d0 fhigh d1 d2 x ftanh F0 r F1 xm d3 d4 proj d5 d6 sp F2 oT F3 v d7 rT",
        "d0 d1 d2 d3 F4 F5 d4 turned d5 x d6 r xm F6 F7 d7 proj sp",
        "fhigh d0 d1 d2 d3 F0 F1 ftanh turned x r xm d4 d5 d6 F2 proj F3 d7 sp",
        "turned d0 x F4 r F5 xm d1 d2 proj d3 d4 d5 sp oT F6 F7 d6 d7 v rT"),
    "vector": (
        "flow b0 gate flog ftop s0 b1 g0 s1 conv b2 g1 s2 b3 g2 b4 s3 low g3 fweights f0 f1 s4 b5 g4 s5 "
        "delta mask b6 g5 s6 b7 g6 s7 g7 xb",
        "f2 fstats f3 b0 gate b1 s0 xsum g0 s1 un b2 g1 b3 f4 s2 s3 conv f5 g2 b4 g3 s4 b5 g4 b6 s5 s6 g5 "
        "b7 g6 s7 low f6 g7 f7 fnorm delta",
        "b0 flow gate flog b1 s0 s1 ftop xsum g0 b2 un g1 b3 s2 lx g2 conv b4 fweights f0 s3 f1 g3 ln b5 s4 "
        "s5 g4 b6 g5 s6 low b7 g6 s7 unx g7 delta",
        "f2 f3 b0 gate conv s0 b1 g0 b2 fstats f4 s1 s2 low g1 b3 g2 f5 b4 s3 s4 g3 delta b5 g4 s5 mask b6 "
        "g5 b7 s6 f6 g6 s7 f7 fnorm g7 xb"),
    "gpsimd": (
        "a1 a2 a3 a4 a5 a6 a7",
        "rms rs a1 froot a2 a3 a4 a5 a6 a7",
        "rms rs lnx a1 a2 a3 rmsx a4 a5 a6 a7",
        "froot a1 a2 a3 a4 a5 a6 a7"),
}


def steps(engine, i):
    for word in ORDER[engine][i].split():
        name = word.rstrip("0123456789")
        yield name, int(word[len(name):] or 0)


def pieces_in(i):
    return sum(n for name, n in steps("tensor", i) if name == "p")


COL, WIDTH = {}, 0
for _name, _w in PACK:
    COL[_name] = (WIDTH, WIDTH + _w)
    WIDTH += _w


def moe_mamba_kernel(nc, x, pack, sel, w1, w2, out):
    fp32, fp32r, u32 = mybir.dt.float32, mybir.dt.float32r, mybir.dt.uint32
    ALU, ACT = mybir.AluOpType, mybir.ActivationFunctionType

    ctx = ExitStack()
    with ctx:
        def sb(name, shape, dt=fp32):
            return ctx.enter_context(nc.sbuf_tensor(name, shape, dt))

        prm = sb("prm", [P, WIDTH])
        raw = sb("raw", [P, E * HID])
        w1h = sb("w1h", [P, E, HID], fp32r)
        w1l = sb("w1l", [P, E, HID], fp32r)
        w2s = sb("w2s", [P, E, HC, D])
        selr = sb("selr", [4 * DS, 2 * DS, P], fp32r)
        gh = sb("gh", [P, E], fp32r)
        gl = sb("gl", [P, E], fp32r)
        inw = sb("inw", [P, 2, 2 * DI])
        tapb = sb("tapb", [P, HALVES])
        A = sb("A", [P, HALVES, DS])
        lgam = sb("lgam", [P, 4])
        powh = sb("powh", [P, TILES])
        epst = sb("epst", [P, TILES])

        def par(name):
            a, b = COL[name]
            return prm[:, a:b]

        MT = prm[:, COL["dist"][0]:COL["dist"][0] + T + P]

        xin = sb("xin", [P, TILES, D])
        stats = sb("stats", [P, TILES, 6])
        mv = sb("mv", [P, TILES, 2])
        rstd = sb("rstd", [P, TILES])
        xn = sb("xn", [P, TILES, D])
        xh = sb("xh", [P, TOK], fp32r)
        xl = sb("xl", [P, TOK], fp32r)
        lg = sb("lg", [P, TILES, E])
        m8 = sb("m8", [P, TILES, 8])
        ix = sb("ix", [P, TILES, 8], u32)
        ixf = sb("ixf", [P, TILES, 8])
        gap = sb("gap", [P, TILES])
        th = sb("th", [P, TILES])
        c01 = sb("c01", [P, 2, TILES])
        hit = sb("hit", [P, 2, TILES, E])
        comb = sb("comb", [P, TILES, E])
        hT = [raw[:, i * HC * TOK:(i + 1) * HC * TOK].rearrange("p (c t) -> p c t", c=HC)
              for i in range(2)]
        xa = sb("xa", [P, TILES, D])
        xb = sb("xb", [P, TILES, D])
        ob = sb("ob", [P, TILES, D])

        xam = sb("xam", [P, TILES, D])
        statm = sb("statm", [P, TILES, 6])
        mvm = sb("mvm", [P, TILES, 2])
        rstdm = sb("rstdm", [P, TILES])
        statr = sb("statr", [P, TILES, 6])
        mvr = sb("mvr", [P, TILES, 2])
        rstdr = sb("rstdr", [P, TILES])
        varr = sb("varr", [P, TILES])
        vr = sb("vr", [P, TILES])
        ln = sb("ln", [P, TILES, D])
        x1 = sb("x1", [P, TILES, D])
        rs = sb("rs", [P, TILES, D])
        un = sb("un", [P, TILES, D])
        uT = sb("uT", [P, TOK])
        xpad = [sb(f"xpad{b}", [P, HALVES, PAD + T]) for b in range(SEQ)]
        xm = [sb(f"xm{b}", [P, HALVES, T]) for b in range(SEQ)]
        sres = [sb(f"sres{b}", [P, HALVES, T]) for b in range(SEQ)]
        bcr = [sb(f"bcr{b}", [4 * DS, T], fp32r) for b in range(SEQ)]
        delta = [sb(f"delta{b}", [P, HALVES, T]) for b in range(SEQ)]
        du = [sb(f"du{b}", [P, HALVES, T]) for b in range(SEQ)]
        acc = [sb(f"acc{b}", [P, DP, HALVES, T]) for b in range(SEQ)]
        dtT = sb("dtT", [DR, T])
        z = sb("z", [P, HALVES, T])
        conv = z
        ez = sb("ez", [P, HALVES, T])
        yg = sb("yg", [P, HALVES, T])
        dA = [sb(f"dA{i}", [P, DP, HALVES, T]) for i in range(4)]
        dbu = [sb(f"dbu{i}", [P, DP, HALVES, T]) for i in range(2)]
        hs = [sb(f"hs{i}", [P, DP, HALVES, T]) for i in range(2)]
        G = [sb(f"G{i}", [P, DP, HALVES, T]) for i in range(NG)]
        oT = sb("oT", [P, 1 + T])
        vt = sb("vt", [P, T // P, D])
        rT = vt[:, :, :].rearrange("p j d -> p (j d)")
        SM = sb("SM", [P, T + P])

        bank = [ctx.enter_context(nc.psum_tensor(n, [P, 512], fp32))
                for n in ("b_out", "b_h0", "b_h1", "b_w0", "b_w1", "b_r0", "b_r1", "b_r2")]
        OUT, H, W, R = bank[0], bank[1:3], bank[3:5], bank[5:8]
        EOUT = (OUT, H[1])

        def sem(name):
            return ctx.enter_context(nc.semaphore(name))

        s_pack, s_w1, s_w2, s_sel = sem("s_pack"), sem("s_w1"), sem("s_w2"), sem("s_sel")
        s_raw_read, s_lg, s_Aexp, s_set_dve, s_set_act, s_exponent, s_prep = (
            sem("s_raw_read"), sem("s_lg"), sem("s_Aexp"), sem("s_set_dve"), sem("s_set_act"),
            sem("s_exponent"), sem("s_prep"))
        s_xin, s_store = sem("s_xin"), sem("s_store")
        f_stats, f_rstd, f_xn, f_xnT, f_split, f_logits, f_lread, f_gap, f_th, f_xh = (
            sem("f_stats"), sem("f_rstd"), sem("f_xn"), sem("f_xnT"), sem("f_split"),
            sem("f_logits"), sem("f_lread"), sem("f_gap"), sem("f_th"), sem("f_xh"))
        f_hmm, f_hact, f_ymm, f_yacc = sem("f_hmm"), sem("f_hact"), sem("f_ymm"), sem("f_yacc")
        g_stats, g_rstd, g_xam, g_ln, g_x1, g_rs, g_xb = (
            sem("g_stats"), sem("g_rstd"), sem("g_xam"), sem("g_ln"), sem("g_x1"), sem("g_rs"), sem("g_xb"))
        g_oTmm, g_oT, g_vmm, g_v, g_smm, g_sm, g_rmm, g_r = (
            sem("g_oTmm"), sem("g_oT"), sem("g_vmm"), sem("g_v"), sem("g_smm"), sem("g_sm"),
            sem("g_rmm"), sem("g_r"))
        q_stats, q_rstd, q_u, q_uTmm, q_uT, q_xz, q_xpad, q_conv, q_xm, q_res = (
            sem("q_stats"), sem("q_rstd"), sem("q_u"), sem("q_uTmm"), sem("q_uT"), sem("q_xz"),
            sem("q_xpad"), sem("q_conv"), sem("q_xm"), sem("q_res"))
        q_xmm, q_bc, q_dt, q_zmm, q_sp, q_delta = (
            sem("q_xmm"), sem("q_bc"), sem("q_dt"), sem("q_zmm"), sem("q_sp"), sem("q_delta"))
        q_dA, q_B, q_C, q_dbu, q_scan, q_G, q_gs, q_yg, q_omm, q_bch = (
            sem("q_dA"), sem("q_B"), sem("q_C"), sem("q_dbu"), sem("q_scan"), sem("q_G"),
            sem("q_gs"), sem("q_yg"), sem("q_omm"), sem("q_bch"))

        def piece(k):
            pair, i = divmod(k, PAIR)
            down, i = divmod(i, 2 * HC)
            return bool(down), 2 * pair + i // HC, i % HC

        def wait(eng, s, value):
            if not isinstance(value, int) or value > 0:
                eng.wait_ge(s, value)

        def both(t):
            return t[:, :].rearrange("p (k t) -> p k t", k=2)

        def turn_no(g, i):
            return 3 * g + max(i - 1, 0)

        def first(g):
            return g if g < 2 else 2 * g - 2

        def second(g):
            return 2 * g + 3 if g < GROUPS - 2 else g + GROUPS

        block = ctx.enter_context(nc.Block())

        @block.sync
        def _(sp):
            xt = x.rearrange("(g j p) d -> g p j d", p=P, j=TILES)
            ot = out.rearrange("(g j p) d -> g p j d", p=P, j=TILES)
            sp.dma_start(prm[:, :], pack).then_inc(s_pack, 16)
            sp.dma_start(xin[:, :, :], xt[0]).then_inc(s_xin, 16)
            sp.dma_start(raw[:, :].rearrange("p (e h) -> p e h", e=E),
                         w1.rearrange("e d h -> d e h")).then_inc(s_w1, 16)
            sp.dma_start(w2s[:, :, :, :].rearrange("p e c d -> p (e c) d"),
                         w2.rearrange("e (c p) d -> p (e c) d", p=P)).then_inc(s_w2, 16)
            sp.wait_ge(s_raw_read, 1)
            sp.dma_start(raw[0:4 * DS, :], sel).then_inc(s_sel, 16)

            def store(g):
                sp.wait_ge(f_yacc, (second(g) + 1) * E)
                sp.dma_start(ot[g], ob[:, :, :]).then_inc(s_store, 16)

            for g in range(GROUPS):
                if g + 1 < GROUPS:
                    sp.wait_ge(f_yacc, first(g) * E + 1)
                    sp.dma_start(xin[:, :, :], xt[g + 1]).then_inc(s_xin, 16)
                if g >= 2:
                    store(g - 2)
            store(GROUPS - 2)
            store(GROUPS - 1)
            sp.wait_ge(s_store, 16 * GROUPS)

        @block.tensor
        def _(pe):
            mm = nc.tensor.matmul
            ident = par("ident")

            def ffn_turn(n):
                pe.wait_ge(f_xn, n + 1)
                wait(pe, f_yacc, n * E)
                for j in range(TILES):
                    last = nc.tensor.transpose(OUT[:, j * P:(j + 1) * P], xn[:, j, :], ident)
                last.then_inc(f_xnT, 1)

            def ffn_gate(n):
                pe.wait_ge(f_split, n + 1)
                wait(pe, f_hact, n * E * HC)
                for j in range(TILES):
                    t = slice(j * P, (j + 1) * P)
                    for k, (a, b) in enumerate(((xh, gh), (xh, gl), (xl, gh), (xl, gl))):
                        last = mm(H[0][:, j * E:(j + 1) * E], a[:, t], b[:, :], start=k == 0, stop=k == 3)
                last.then_inc(f_logits, 1)

            def ffn_up(n, e, c):
                i = e * HC + c
                if i == 0:
                    pe.wait_ge(f_lread, n + 1)
                else:
                    wait(pe, f_hact, n * E * HC + i - 1)
                if e % 2 == 0 and e > 0 and c == 1:
                    pe.wait_ge(f_yacc, n * E + e)
                w = slice(c * P, (c + 1) * P)
                h = H[i % 2][:, :]
                mm(h, w1h[:, e, w], xh[:, :], start=True, stop=False)
                mm(h, w1h[:, e, w], xl[:, :], start=False, stop=False)
                mm(h, w1l[:, e, w], xh[:, :], start=False, stop=True).then_inc(f_hmm, 1)

            def ffn_down(n, e, j):
                if j == 0:
                    pe.wait_ge(f_hact, (n * E + e + 1) * HC)
                    wait(pe, f_yacc, n * E + e - 1)
                for c in range(HC):
                    last = mm(EOUT[e % 2][:, j * D:(j + 1) * D], hT[e % 2][:, c, j * P:(j + 1) * P],
                              w2s[:, e, c, :], start=c == 0, stop=c == HC - 1)
                if j == TILES - 1:
                    last.then_inc(f_ymm, 1)

            def turn(g, i):
                tiles = range(TILES) if i == 0 else range(T // P)
                pe.wait_ge(q_u, turn_no(g, i) + 1)
                wait(pe, q_sp, 4 * g + i)
                for j in tiles:
                    last = nc.tensor.transpose(W[1][:, j * P:(j + 1) * P],
                                               un[:, (i % 2 * (T // P) if i else 0) + j, :], ident)
                last.then_inc(q_uTmm, 1)

            def in_proj(g, i):
                q, b = 4 * g + i, i % 2
                pe.wait_ge(q_uT, turn_no(g, i) + 1)
                if i == 1:
                    pe.wait_ge(q_sp, q)
                    wait(pe, g_xb, 2 * g - 1)
                for w in range(2):
                    for k in range(HALVES):
                        p = (w * HALVES + k) * P
                        last = mm(W[w][:, k * T:(k + 1) * T], inw[:, i // 2, p:p + P],
                                  uT[:, b * T:(b + 1) * T], start=True, stop=True)
                    last.then_inc(q_xz, 1)

            def x_proj(g, i):
                q, b = 4 * g + i, i % 2
                pe.wait_ge(q_xm, 2 * q + 2)
                for o, w in ((W[0][0:DR, 0:T], "xp_dt"), (W[0][0:4 * DS, T:], "xp_bc")):
                    wd = par(w)
                    n = o.shape[0]
                    for k in range(HALVES):
                        last = mm(o, wd[:, k * n:(k + 1) * n], xm[b][:, k, :], start=k == 0, stop=k == HALVES - 1)
                last.then_inc(q_xmm, 1)

            def dt_proj(g, i):
                q = 4 * g + i
                pe.wait_ge(q_dt, q + 1)
                for k in range(HALVES):
                    last = mm(W[1][:, k * T:(k + 1) * T], par("dt_w")[0:DR, k * P:(k + 1) * P], dtT[:, :],
                              start=True, stop=True)
                last.then_inc(q_zmm, 1)

            def spread(g, i, t):
                q, b = 4 * g + i, i % 2
                if t == 0:
                    pe.wait_ge(q_bc, q + 1)
                ring = lambda i, t: (t + SHIFT[i]) % RING
                if t >= RING:
                    kind, j = SPREAD[t - RING]
                    pe.wait_ge(q_G if kind else q_dbu, q * NP + j + 1)
                else:
                    kind, j = next(SPREAD[o] for o in range(2 * NP - RING, 2 * NP)
                                   if ring((i - 1) % 4, o) == ring(i, t))
                    if not isinstance(g, int) or q > 0:
                        pe.wait_ge(q_G if kind else q_dbu, q * NP - NP + j + 1)
                kind, j = SPREAD[t]
                for d in range(DP):
                    last = mm(R[ring(i, t)][:, d * T:(d + 1) * T], selr[:, kind * DS + DP * j + d, :], bcr[b][:, :],
                              start=True, stop=True)
                last.then_inc(q_C if kind else q_B, 1)

            def out_proj(o, j, stop):
                for k in range(HALVES):
                    mm(o, yg[:, k, j * P:(j + 1) * P], par("out_w")[:, k * D:(k + 1) * D], start=k == 0, stop=False)
                return mm(o, par("ones_row"), par("out_b_row"), start=False, stop=stop)

            def first_out(g, i):
                q = 4 * g + i
                pe.wait_ge(q_yg, q + 1)
                for j in range(T // P):
                    last = out_proj(W[0][:, j * D:(j + 1) * D], j, True)
                last.then_inc(q_omm, 1)

            def memory_1(g, b, head):
                q = 4 * g + 2 + b
                pe.wait_ge(q_yg, q + 1)
                if head:
                    pe.wait_ge(q_bc, q + 3)
                for k in range(HALVES):
                    last = mm(W[0][:, 0:T], par("out_w")[:, k * D:(k + 1) * D], yg[:, k, :],
                              start=k == 0, stop=k == HALVES - 1)
                last.then_inc(g_oTmm, 1)

            def memory_2(g, b):
                pe.wait_ge(g_oT, 2 * g + b + 1)
                for j in range(T // P):
                    last = mm(W[0][:, T + j * D:T + (j + 1) * D], oT[:, 1 + j * P:1 + (j + 1) * P], par("write_w"),
                              start=True, stop=True)
                last.then_inc(g_vmm, 1)
                mm(W[1][:, 0:T], oT[:, 0:P], oT[:, 1:1 + T], start=True, stop=True)
                mm(W[1][:, T:T + P], oT[:, P:T], oT[:, 1 + P:1 + T], start=True, stop=True).then_inc(g_smm, 1)

            def memory_3(g, b):
                pe.wait_ge(g_v, 2 * g + b + 1)
                pe.wait_ge(g_sm, 2 * g + b + 1)
                mm(W[0][:, 0:P], vt[:, 0, :], SM[:, 0:P], start=True, stop=True)
                mm(W[0][:, P:T], vt[:, 0, :], SM[:, P:T], start=True, stop=False)
                mm(W[0][:, P:T], vt[:, 1, :], SM[:, T:T + P], start=False, stop=True).then_inc(g_rmm, 1)

            def memory_4(g, b):
                pe.wait_ge(g_r, 2 * g + b + 1)
                for j in range(T // P):
                    o = W[1][:, j * D:(j + 1) * D]
                    out_proj(o, j, False)
                    last = mm(o, rT[:, j * P:(j + 1) * P], par("read_w"), start=False, stop=True)
                last.then_inc(q_omm, 1)

            def slot(g, i, tail, head, n, nx):
                k = pieces_in(i - 1) if i % 2 else 0
                for name, num in steps("tensor", i):
                    if name == "t":
                        spread(g, i, num)
                    elif name == "p":
                        if n is not None:
                            for x in range(k, k + num):
                                down, e, part = piece(x)
                                (ffn_down if down else ffn_up)(n, e, part)
                        k += num
                    elif name in ("fturn", "fgate"):
                        if n is not None:
                            (ffn_turn if name == "fturn" else ffn_gate)(n)
                    elif name == "turng":
                        if head:
                            turn(head[0], 0)
                    elif name in ("in", "xp", "dt", "turn"):
                        if head:
                            {"in": in_proj, "xp": x_proj, "dt": dt_proj, "turn": turn}[name](*head)
                    elif tail:
                        if name == "out":
                            first_out(*tail)
                        elif num == 1:
                            memory_1(tail[0], tail[1] - 2, head)
                        else:
                            (memory_2, memory_3, memory_4)[num - 2](tail[0], tail[1] - 2)
                assert i % 2 == 0 or k == PIECES

            def alone(n):
                ffn_turn(n)
                ffn_gate(n)
                for x in range(PIECES):
                    down, e, part = piece(x)
                    (ffn_down if down else ffn_up)(n, e, part)

            def start():
                alone(first(0))
                turn(0, 0)
                in_proj(0, 0)
                x_proj(0, 0)
                dt_proj(0, 0)

            def finish():
                tail = (GROUPS - 1, 1)
                memory_1(*tail, None)
                memory_2(*tail)
                memory_3(*tail)
                memory_4(*tail)
                alone(second(GROUPS - 1))

            pe.wait_ge(s_pack, 16)
            pe.wait_ge(s_w2, 16)
            pe.wait_ge(s_set_dve, 1)
            def run(g, n1, n2, n3, is_last):
                for i in range(4):
                    tail = (g, i - 1) if i else None if isinstance(g, int) and g == 0 else (g - 1, 3)
                    head = (g, i + 1) if i < 3 else None if is_last else (g + 1, 0)
                    slot(g, i, tail, head, (n1, n2)[i // 2], (n2, n3)[i // 2])

            start()
            run(0, first(1), None, first(2), False)
            with pe.Fori(1, GROUPS - 2) as g:
                run(g, g * 2, g * 2 + 1, g * 2 + 2, False)
            run(GROUPS - 2, first(GROUPS - 1), second(GROUPS - 3), None, False)
            run(GROUPS - 1, None, second(GROUPS - 2), None, True)
            finish()

        @block.scalar
        def _(act):
            do = nc.scalar.activation

            act.wait_ge(s_pack, 16)
            do(lgam[:, 0:1], par("decay"), ACT.Abs)
            act.drain()
            do(lgam[:, 1:2], lgam[:, 0:1], ACT.Exp, scale=-1.0)
            act.drain()
            do(lgam[:, 2:3], lgam[:, 1:2], ACT.Ln, bias=1.0).then_inc(s_lg, 1)
            do(A[:, :, :], par("A_log").rearrange("p (h s) -> p h s", s=DS), ACT.Exp).then_inc(s_Aexp, 1)
            act.wait_ge(s_exponent, 1)
            do(MT[:, 0:T], par("dist"), ACT.Exp, scale=lgam[:, 3:4]).then_inc(s_set_act, 1)
            act.wait_ge(s_set_dve, 1)

            def ffn_high(n):
                act.wait_ge(f_xnT, n + 1)
                wait(act, f_hmm, n * E * HC)
                do(xh[:, :], OUT[:, :], ACT.Copy).then_inc(f_xh, 1)

            def ffn_gate(n):
                act.wait_ge(f_gap, n + 1)
                do(th[:, :], gap[:, :], ACT.Tanh, scale=0.5).then_inc(f_th, 1)

            def ffn_silu(n, e):
                for c in range(HC):
                    i = e * HC + c
                    if c == 0:
                        wait(act, f_ymm, n * E + e - 1)
                    act.wait_ge(f_hmm, n * E * HC + i + 1)
                    do(hT[e % 2][:, c, :], H[i % 2][:, :], ACT.Silu).then_inc(f_hact, 1)

            def turned(g, i):
                act.wait_ge(q_uTmm, turn_no(g, i) + 1)
                if i == 0:
                    wait(act, q_xz, 8 * g)
                    do(uT[:, :], W[1][:, :], ACT.Copy).then_inc(q_uT, 1)
                else:
                    wait(act, q_xz, 2 * (4 * g + i - 1))
                    b = i % 2
                    do(uT[:, b * T:(b + 1) * T], W[1][:, 0:T], ACT.Copy).then_inc(q_uT, 1)

            def conv_input(g, i):
                q, b = 4 * g + i, i % 2
                act.wait_ge(q_xz, 2 * q + 1)
                wait(act, q_delta, q)
                for k in range(HALVES):
                    do(conv[:, k, :], W[0][:, k * T:(k + 1) * T], ACT.Identity,
                       scale=par("conv_w")[:, k * DC + PAD:k * DC + DC], bias=tapb[:, k:k + 1])
                for k in range(HALVES):
                    do(xpad[b][:, k, PAD:], W[0][:, k * T:(k + 1) * T], ACT.Identity,
                       bias=par("in_b")[:, k:k + 1]).then_inc(q_xpad, 1)

            def gate_input(g, i):
                q, b = 4 * g + i, i % 2
                wait(act, q_yg, q - 1)
                act.wait_ge(q_xz, 2 * q + 2)
                for k in range(HALVES):
                    do(sres[b][:, k, :], W[1][:, k * T:(k + 1) * T], ACT.Silu,
                       bias=par("in_b")[:, 2 + k:3 + k]).then_inc(q_res, 1)

            def conv_silu(g, i):
                q, b = 4 * g + i, i % 2
                for k in range(HALVES):
                    act.wait_ge(q_conv, 2 * q + k + 1)
                    do(xm[b][:, k, :], conv[:, k, :], ACT.Silu, bias=par("conv_b")[:, k:k + 1]).then_inc(q_xm, 1)

            def projections(g, i):
                q, b = 4 * g + i, i % 2
                act.wait_ge(q_xmm, q + 1)
                wait(act, q_zmm, q)
                do(dtT[:, :], W[0][0:DR, 0:T], ACT.Copy).then_inc(q_dt, 1)
                wait(act, q_C, (q - 1) * NP)
                do(bcr[b][:, :], W[0][0:4 * DS, T:], ACT.Copy).then_inc(q_bch, 1)

            def softplus(g, i):
                q = 4 * g + i
                act.wait_ge(q_zmm, q + 1)
                wait(act, q_delta, q)
                for o, f in ((ez, ACT.Abs), (z, ACT.Identity)):
                    for k in range(HALVES):
                        do(o[:, k, :], W[1][:, k * T:(k + 1) * T], f, bias=par("dt_b")[:, k:k + 1])
                act.drain()
                do(ez[:, :, :], ez[:, :, :], ACT.Exp, scale=-1.0)
                act.drain()
                do(ez[:, :, :], ez[:, :, :], ACT.Ln, bias=1.0).then_inc(q_sp, 1)

            def decays(g, i, j):
                q, b = 4 * g + i, i % 2
                if j == 0:
                    act.wait_ge(q_delta, q + 1)
                wait(act, q_scan, q * NP + j - 3)
                for d in range(DP):
                    s = DP * j + d
                    for k in range(HALVES):
                        last = do(dA[j % 4][:, d, k, 1:], delta[b][:, k, 1:], ACT.Exp, scale=A[:, k, s:s + 1])
                last.then_inc(q_dA, 1)

            def memory_out(g, b):
                act.wait_ge(g_oTmm, 2 * g + b + 1)
                do(oT[:, 1:], W[0][:, 0:T], ACT.Identity, bias=par("out_b")).then_inc(g_oT, 1)

            def memory_v(g, b):
                act.wait_ge(g_vmm, 2 * g + b + 1)
                do(vt[:, :, :], W[0][:, T:].rearrange("p (j d) -> p j d", d=D), ACT.Copy).then_inc(g_v, 1)

            def memory_reads(g, b):
                act.wait_ge(g_rmm, 2 * g + b + 1)
                do(rT[:, :], W[0][:, 0:T], ACT.Copy).then_inc(g_r, 1)

            def slot(g, i, tail, head, n, nx):
                for name, num in steps("scalar", i):
                    if name == "d":
                        decays(g, i, num)
                    elif name == "F":
                        if n is not None:
                            ffn_silu(n, num)
                    elif name == "ftanh":
                        if n is not None:
                            ffn_gate(n)
                    elif name == "fhigh":
                        if n is not None:
                            ffn_high(n)
                    elif name in ("oT", "v", "rT"):
                        if tail:
                            {"oT": memory_out, "v": memory_v, "rT": memory_reads}[name](tail[0], tail[1] - 2)
                    elif head:
                        {"turned": turned, "x": conv_input, "r": gate_input,
                         "xm": conv_silu, "proj": projections, "sp": softplus}[name](*head)

            def alone(n):
                ffn_high(n)
                for e in range(E):
                    ffn_silu(n, e)
                    if e == 0:
                        ffn_gate(n)

            def start():
                alone(first(0))
                turned(0, 0)
                conv_input(0, 0)
                gate_input(0, 0)
                conv_silu(0, 0)
                projections(0, 0)
                softplus(0, 0)

            def finish():
                tail = (GROUPS - 1, 1)
                memory_out(*tail)
                memory_v(*tail)
                memory_reads(*tail)
                alone(second(GROUPS - 1))

            def run(g, n1, n2, n3, is_last):
                for i in range(4):
                    tail = (g, i - 1) if i else None if isinstance(g, int) and g == 0 else (g - 1, 3)
                    head = (g, i + 1) if i < 3 else None if is_last else (g + 1, 0)
                    slot(g, i, tail, head, (n1, n2)[i // 2], (n2, n3)[i // 2])

            start()
            run(0, first(1), None, first(2), False)
            with act.Fori(1, GROUPS - 2) as g:
                run(g, g * 2, g * 2 + 1, g * 2 + 2, False)
            run(GROUPS - 2, first(GROUPS - 1), second(GROUPS - 3), None, False)
            run(GROUPS - 1, None, second(GROUPS - 2), None, True)
            finish()

        @block.vector
        def _(dve):
            V = nc.vector

            def norm_stats(src, st, agg, tiles=range(TILES)):
                for j in tiles:
                    V.bn_stats(st[:, j, :], src[:, j, :])
                dve.drain()
                for j in tiles:
                    last = V.bn_aggr(agg[:, j, :], st[:, j, :])
                return last

            V.memset(oT[:, 0:1], 0.0)
            for b in range(SEQ):
                V.memset(xpad[b][:, :, 0:PAD], 0.0)
            for i in range(4):
                V.memset(dA[i][:, :, :, 0:1], 0.0)
            dve.wait_ge(s_pack, 16)
            for m, nw in enumerate(("norm1", "norm2")):
                V.tensor_scalar(inw[:, m, :], par("in_w"), par(nw), None, ALU.mult)
            for k in range(HALVES):
                V.tensor_tensor(tapb[:, k:k + 1], par("in_b")[:, k:k + 1],
                                par("conv_w")[:, k * DC + PAD:k * DC + DC], ALU.mult)
            V.tensor_copy(gh[:, :], par("gate"))
            V.tensor_scalar(par("read_w"), par("read_w"), 0.1, None, ALU.mult)
            dve.drain()
            V.tensor_tensor(gl[:, :], par("gate"), gh[:, :].bitcast(fp32), ALU.subtract)
            dve.wait_ge(s_lg, 1)
            V.tensor_scalar(lgam[:, 0:1], par("decay"), 0.0, None, ALU.min)
            dve.drain()
            V.tensor_tensor(lgam[:, 3:4], lgam[:, 0:1], lgam[:, 2:3], ALU.subtract).then_inc(s_exponent, 1)
            dve.wait_ge(s_w1, 16)
            rv = raw[:, :].rearrange("p (e h) -> p e h", e=E)
            V.tensor_copy(w1h[:, :, :], rv)
            dve.drain()
            V.tensor_tensor(w1l[:, :, :], rv, w1h[:, :, :].bitcast(fp32), ALU.subtract).then_inc(s_raw_read, 1)
            dve.wait_ge(s_Aexp, 1)
            V.tensor_scalar(A[:, :, :], A[:, :, :], -1.0, None, ALU.mult)
            dve.wait_ge(s_set_act, 1)
            V.tensor_tensor(MT[:, 0:T], MT[:, 0:T], par("causal"), ALU.mult)
            dve.drain()
            V.tensor_copy(MT[:, T:T + P], MT[:, 0:P])
            dve.wait_ge(s_sel, 16)
            V.tensor_copy(selr[:, :, :], raw[0:4 * DS, :].rearrange("p (i m) -> p i m", m=P))
            dve.drain()
            V.memset(gap[:, :], 0.0).then_inc(s_set_dve, 1)

            def ffn_stats(f):
                n, src, dst, g, is_first = f
                if is_first:
                    dve.wait_ge(s_xin, g * 16 + 16)
                else:
                    dve.wait_ge(g_xb, SEQ * (g + 1))
                norm_stats(src, stats, mv).then_inc(f_stats, 1)

            def ffn_norm(f):
                n, src, dst, g, is_first = f
                dve.wait_ge(f_rstd, n + 1)
                wait(dve, f_xnT, n)
                for j in range(TILES):
                    last = V.tensor_scalar(xn[:, j, :], src[:, j, :], mv[:, j, 0:1], rstd[:, j:j + 1],
                                           ALU.subtract, ALU.mult)
                last.then_inc(f_xn, 1)

            def ffn_low(f):
                n = f[0]
                dve.wait_ge(f_xh, n + 1)
                wait(dve, f_hmm, n * E * HC)
                V.tensor_tensor(xl[:, :], OUT[:, :], xh[:, :].bitcast(fp32), ALU.subtract).then_inc(f_split, 1)

            def ffn_logits(f):
                dve.wait_ge(f_logits, f[0] + 1)
                V.tensor_copy(lg[:, :, :], H[0][:, 0:TILES * E].rearrange("p (j e) -> p j e", e=E))\
                    .then_inc(f_lread, 1)

            def ffn_top(f):
                dve.drain()
                for j in range(TILES):
                    V.max(m8[:, j, :], lg[:, j, :])
                dve.drain()
                V.tensor_tensor(gap[:, :], m8[:, :, 0], m8[:, :, 1], ALU.subtract).then_inc(f_gap, 1)
                for j in range(TILES):
                    V.max_index(ix[:, j, :], m8[:, j, :], lg[:, j, :])
                dve.drain()
                V.tensor_copy(ixf[:, :, :], ix[:, :, :])

            def ffn_weights(f):
                dve.wait_ge(f_th, f[0] + 1)
                V.tensor_scalar(c01[:, 0, :], th[:, :], 0.25, 0.25, ALU.mult, ALU.add)
                V.tensor_scalar(c01[:, 1, :], th[:, :], -0.25, 0.25, ALU.mult, ALU.add)
                dve.drain()
                iota = par("iota").unsqueeze(1).broadcast_to([P, TILES, E])
                for k in range(2):
                    V.tensor_tensor(hit[:, k, :, :], iota, ixf[:, :, k:k + 1].broadcast_to([P, TILES, E]),
                                    ALU.is_equal)
                dve.drain()
                for k in range(2):
                    V.tensor_tensor(hit[:, k, :, :], hit[:, k, :, :],
                                    c01[:, k, :].unsqueeze(2).broadcast_to([P, TILES, E]), ALU.mult)
                dve.drain()
                V.tensor_tensor(comb[:, :, :], hit[:, 0, :, :], hit[:, 1, :, :], ALU.add)
                dve.drain()

            def ffn_sum(f, e):
                n, src, dst, g, is_first = f
                dve.wait_ge(f_ymm, n * E + e + 1)
                wait(dve, f_yacc, n * E + e)
                if e == 0:
                    wait(dve, *((g_xam, g) if is_first else (s_store, g * 16)))
                for j in range(TILES):
                    last = V.scalar_tensor_tensor(
                        out=dst[:, j, :], in0=EOUT[e % 2][:, j * D:(j + 1) * D],
                        scalar=comb[:, j, e:e + 1], in1=(src if e == 0 else dst)[:, j, :],
                        op0=ALU.mult, op1=ALU.add)
                last.then_inc(f_yacc, 1)

            def mixer_norm_stats(g):
                dve.drain()
                norm_stats(xa, statm, mvm).then_inc(g_stats, 1)

            def mixer_norm(g):
                dve.wait_ge(g_rstd, g + 1)
                for j in range(TILES):
                    last = V.tensor_scalar(ln[:, j, :], xa[:, j, :], mvm[:, j, 0:1], rstdm[:, j:j + 1],
                                           ALU.subtract, ALU.mult)
                last.then_inc(g_ln, 1)

            def square_stats(src, tiles):
                norm_stats(src, statr, mvr, tiles)
                dve.drain()
                for j in tiles:
                    last = V.scalar_tensor_tensor(out=varr[:, j:j + 1], in0=mvr[:, j, 0:1], scalar=mvr[:, j, 0:1],
                                                  in1=mvr[:, j, 1:2], op0=ALU.mult, op1=ALU.add)
                last.then_inc(q_stats, 1)

            def square_norm(g, i, src, tiles):
                dve.wait_ge(q_rstd, turn_no(g, i) + 1)
                wait(dve, q_uTmm, turn_no(g, i))
                for j in tiles:
                    last = V.tensor_scalar(un[:, j, :], src[:, j, :], rstdr[:, j:j + 1], None, ALU.mult)
                last.then_inc(q_u, 1)

            def of_seq(b):
                return range(b * T // P, (b + 1) * T // P)

            def conv_taps(g, i):
                q, b = 4 * g + i, i % 2
                cw = par("conv_w")
                for j in range(PAD):
                    if j > 0:
                        dve.drain()
                    for k in range(HALVES):
                        if j == 0:
                            dve.wait_ge(q_xpad, 2 * q + k + 1)
                        last = V.scalar_tensor_tensor(
                            out=conv[:, k, :], in0=xpad[b][:, k, j:j + T], scalar=cw[:, k * DC + j:k * DC + j + 1],
                            in1=conv[:, k, :], op0=ALU.mult, op1=ALU.add)
                        if j == PAD - 1:
                            last.then_inc(q_conv, 1)

            def low_part(g, i):
                q, b = 4 * g + i, i % 2
                dve.wait_ge(q_bch, q + 1)
                lo = slice(2 * DS, 4 * DS)
                V.tensor_tensor(bcr[b][lo, :], W[0][lo, T:], bcr[b][lo, :].bitcast(fp32), ALU.subtract)\
                    .then_inc(q_bc, 1)

            def delta_u(g, i):
                q, b = 4 * g + i, i % 2
                dve.wait_ge(q_sp, q + 1)
                V.scalar_tensor_tensor(out=delta[b][:, :, :], in0=z[:, :, :], scalar=0.0, in1=ez[:, :, :],
                                       op0=ALU.max, op1=ALU.add).then_inc(q_delta, 1)
                dve.wait_ge(q_delta, q + 1)
                V.tensor_tensor(du[b][:, :, :], delta[b][:, :, :], xm[b][:, :, :], ALU.mult)
                dve.drain()

            def spread_rows(i, tile):
                return both(R[(SPREAD.index(tile) + SHIFT[i]) % RING]).unsqueeze(2).broadcast_to([P, DP, HALVES, T])

            def flat(b):
                return b[:, :, :, :].rearrange("p d h t -> p (d h t)")

            def scan_input(g, i, j):
                q = 4 * g + i
                dve.wait_ge(q_B, q * NP + j + 1)
                wait(dve, q_scan, q * NP + j - 1)
                V.tensor_tensor(dbu[j % 2][:, :, :, :],
                                du[i % 2][:, :, :].unsqueeze(1).broadcast_to([P, DP, HALVES, T]),
                                spread_rows(i, (0, j)), ALU.mult).then_inc(q_dbu, 1)

            def scan(g, i, j):
                q = 4 * g + i
                dve.wait_ge(q_dA, q * NP + j + 1)
                dve.wait_ge(q_dbu, q * NP + j + 1)
                wait(dve, q_G, q * NP + j - 1)
                V.tensor_tensor_scan(flat(hs[j % 2]), flat(dA[j % 4]), flat(dbu[j % 2]), 0.0, ALU.mult, ALU.add)\
                    .then_inc(q_scan, 1)

            def scan_output(g, i, j):
                q = 4 * g + i
                dve.wait_ge(q_C, q * NP + j + 1)
                dve.wait_ge(q_scan, q * NP + j + 1)
                last = j - NG if j >= NG else max(p for p in range(NP) if p % NG == j) - NP
                wait(dve, q_gs, q * (NP - 1) + (max(last, 1) if last >= 0 else last + 1))
                V.tensor_tensor(G[j % NG][:, :, :, :], hs[j % 2][:, :, :, :], spread_rows(i, (1, j)), ALU.mult)\
                    .then_inc(q_G, 1)

            def gate_y(g, i):
                q, b = 4 * g + i, i % 2
                dve.wait_ge(q_gs, (q + 1) * (NP - 1))
                dve.wait_ge(q_res, 2 * q + 2)
                wait(dve, q_omm, q)
                V.tensor_tensor(yg[:, :, :], acc[b][:, 0, :, :], acc[b][:, 1, :, :], ALU.add)
                dve.drain()
                for k in range(HALVES):
                    V.scalar_tensor_tensor(out=yg[:, k, :], in0=xm[b][:, k, :], scalar=par("D_ssm")[:, k:k + 1],
                                           in1=yg[:, k, :], op0=ALU.mult, op1=ALU.add)
                dve.drain()
                V.tensor_tensor(yg[:, :, :], yg[:, :, :], sres[b][:, :, :], ALU.mult).then_inc(q_yg, 1)

            def out_tiles(w):
                return w[:, 0:T].rearrange("p (j d) -> p j d", d=D)

            def first_sum(g, b):
                tiles = slice(b * T // P, (b + 1) * T // P)
                dve.wait_ge(q_omm, 4 * g + b + 1)
                wait(dve, g_rs, 2 * g + b - 1)
                V.tensor_tensor(x1[:, tiles, :], out_tiles(W[0]), ln[:, tiles, :], ALU.add).then_inc(g_x1, 1)
                dve.wait_ge(g_x1, 2 * g + b + 1)
                square_stats(x1, of_seq(b))

            def masked(g, b):
                dve.wait_ge(g_smm, 2 * g + b + 1)
                V.tensor_tensor(SM[:, :], W[1][:, 0:T + P], MT[:, :], ALU.mult).then_inc(g_sm, 1)

            def mixer_sum(g, b):
                tiles = slice(b * T // P, (b + 1) * T // P)
                dve.wait_ge(q_omm, 4 * g + 2 + b + 1)
                dve.wait_ge(g_rs, 2 * g + b + 1)
                V.tensor_tensor(xb[:, tiles, :], out_tiles(W[1]), rs[:, tiles, :], ALU.add).then_inc(g_xb, 1)

            def slot(g, i, tail, head, f, fx, nxt):
                ffn_steps = {"flog": ffn_logits, "ftop": ffn_top, "fweights": ffn_weights, "flow": ffn_low}
                next_steps = {"fstats": ffn_stats, "fnorm": ffn_norm}
                for name, num in steps("vector", i):
                    if name == "b":
                        scan_input(g, i, num)
                    elif name == "s":
                        scan(g, i, num)
                    elif name == "g":
                        scan_output(g, i, num)
                    elif name == "f":
                        if f:
                            ffn_sum(f, num)
                    elif name in ffn_steps:
                        if f:
                            ffn_steps[name](f)
                    elif name in next_steps:
                        if fx:
                            next_steps[name](fx)
                    elif name in ("lx", "ln", "unx"):
                        if nxt is not None:
                            if name == "lx":
                                mixer_norm_stats(nxt)
                            elif name == "ln":
                                mixer_norm(nxt)
                            else:
                                dve.wait_ge(g_ln, nxt + 1)
                                square_norm(nxt, 0, ln, range(TILES))
                    elif name in ("gate", "xsum", "mask", "xb"):
                        if tail and name == "gate":
                            gate_y(*tail)
                        elif tail:
                            {"xsum": first_sum, "mask": masked, "xb": mixer_sum}[name](tail[0], tail[1] % 2)
                    elif name == "un":
                        square_norm(*head, x1, of_seq(head[1] % 2))
                    elif head:
                        {"conv": conv_taps, "low": low_part, "delta": delta_u}[name](*head)

            def alone(f):
                ffn_stats(f)
                ffn_norm(f)
                ffn_low(f)
                ffn_logits(f)
                ffn_top(f)
                ffn_weights(f)
                for e in range(E):
                    ffn_sum(f, e)

            def start():
                alone((first(0), xin, xa, 0, True))
                f = (first(1), xin, xa, 1, True)
                mixer_norm_stats(0)
                ffn_stats(f)
                mixer_norm(0)
                ffn_norm(f)
                dve.wait_ge(g_ln, 1)
                square_norm(0, 0, ln, range(TILES))
                conv_taps(0, 0)
                low_part(0, 0)
                delta_u(0, 0)

            def finish():
                gate_y(GROUPS - 1, 3)
                masked(GROUPS - 1, 1)
                mixer_sum(GROUPS - 1, 1)
                alone((second(GROUPS - 1), xb, ob, GROUPS - 1, False))

            def run(g, n1, n2, n3, is_last):
                f1 = n1 is not None and (n1, xin, xa, g + 1, True)
                f2 = n2 is not None and (n2, xb, ob, g - 1, False)
                f3 = n3 is not None and (n3, xin, xa, g + 2, True)
                for i in range(4):
                    tail = (g, i - 1) if i else None if isinstance(g, int) and g == 0 else (g - 1, 3)
                    head = (g, i + 1) if i < 3 else None if is_last else (g + 1, 0)
                    slot(g, i, tail, head, (f1, f2)[i // 2], (f2, f3)[i // 2], None if is_last else g + 1)

            start()
            run(0, first(1), None, first(2), False)
            with dve.Fori(1, GROUPS - 2) as g:
                run(g, g * 2, g * 2 + 1, g * 2 + 2, False)
            run(GROUPS - 2, first(GROUPS - 1), second(GROUPS - 3), None, False)
            run(GROUPS - 1, None, second(GROUPS - 2), None, True)
            finish()

        @block.gpsimd
        def _(pool):
            Q = nc.gpsimd
            Q.memset(powh[:, :], -0.5)
            Q.memset(epst[:, :], EPS)
            pool.drain()

            def root(v, r, tiles=slice(0, TILES)):
                Q.tensor_tensor(r[:, tiles], v, epst[:, tiles], ALU.add)
                pool.drain()
                return Q.tensor_tensor(r[:, tiles], r[:, tiles], powh[:, tiles], ALU.pow)

            def ffn_root(n):
                pool.wait_ge(f_stats, n + 1)
                root(mv[:, :, 1], rstd).then_inc(f_rstd, 1)

            def mixer_root(g):
                pool.wait_ge(g_stats, g + 1)
                root(mvm[:, :, 1], rstdm).then_inc(g_rstd, 1)
                Q.tensor_scalar(xam[:, :, :], xa[:, :, :], 1.0, 0.0, ALU.mult, ALU.add).then_inc(g_xam, 1)

            def entry_root(g):
                pool.wait_ge(g_rstd, g + 1)
                Q.tensor_tensor(vr[:, :], mvm[:, :, 1], rstdm[:, :], ALU.mult)
                pool.drain()
                Q.tensor_tensor(vr[:, :], vr[:, :], rstdm[:, :], ALU.mult)
                pool.drain()
                wait(pool, q_u, 3 * g)
                root(vr[:, :], rstdr).then_inc(q_rstd, 1)

            def mamba_root(g, i, tiles):
                pool.wait_ge(q_stats, 2 * g + i - 1)
                root(varr[:, tiles], rstdr, tiles).then_inc(q_rstd, 1)

            def pair_sum(g, i, j):
                q, b = 4 * g + i, i % 2
                pool.wait_ge(q_G, q * NP + j + 1)
                if j == 1:
                    wait(pool, q_yg, q - 1)
                else:
                    pool.wait_ge(q_gs, q * (NP - 1) + j - 1)
                Q.tensor_tensor(acc[b][:, :, :, :], (G[0] if j == 1 else acc[b])[:, :, :, :],
                                G[j % NG][:, :, :, :], ALU.add).then_inc(q_gs, 1)

            def residual(g, b):
                tiles = slice(b * T // P, (b + 1) * T // P)
                pool.wait_ge(g_x1, 2 * g + b + 1)
                wait(pool, g_xb, 2 * g + b - 1)
                Q.tensor_tensor(rs[:, tiles, :], xam[:, tiles, :], x1[:, tiles, :], ALU.add).then_inc(g_rs, 1)

            def slot(g, i, tail, head, n, nx, nxt):
                for name, num in steps("gpsimd", i):
                    if name == "a":
                        pair_sum(g, i, num)
                    elif name == "rms":
                        b = head[1] % 2
                        mamba_root(*head, slice(b * T // P, (b + 1) * T // P))
                    elif name == "rs":
                        residual(tail[0], tail[1])
                    elif name == "froot":
                        if nx is not None:
                            ffn_root(nx)
                    elif nxt is not None:
                        if name == "lnx":
                            mixer_root(nxt)
                        else:
                            entry_root(nxt)

            def start():
                ffn_root(first(0))
                mixer_root(0)
                ffn_root(first(1))
                entry_root(0)

            def finish():
                ffn_root(second(GROUPS - 1))

            def run(g, n1, n2, n3, is_last):
                for i in range(4):
                    tail = (g, i - 1) if i else None if isinstance(g, int) and g == 0 else (g - 1, 3)
                    head = (g, i + 1) if i < 3 else None if is_last else (g + 1, 0)
                    slot(g, i, tail, head, (n1, n2)[i // 2], (n2, n3)[i // 2], None if is_last else g + 1)

            start()
            run(0, first(1), None, first(2), False)
            with pool.Fori(1, GROUPS - 2) as g:
                run(g, g * 2, g * 2 + 1, g * 2 + 2, False)
            run(GROUPS - 2, first(GROUPS - 1), second(GROUPS - 3), None, False)
            run(GROUPS - 1, None, second(GROUPS - 2), None, True)
            finish()


def kernel(**inputs):
    import numpy as np
    import concourse.bacc as bacc
    from concourse.bass_utils import run_bass_kernel_spmd

    def a(name):
        return np.asarray(inputs["L0_" + name])

    def rows(m):
        return m.reshape(-1, P, m.shape[1]).transpose(1, 0, 2).reshape(P, -1)

    def fill(m, r=P):
        return np.concatenate([m, np.zeros((r - m.shape[0], m.shape[1]), m.dtype)], 0)

    t, s = np.arange(T)[None, :], np.arange(P)[:, None]
    xp = a("attn_x_proj_w")
    bc = np.concatenate([xp[DR:]] * 2, 0).T
    ob = a("attn_out_proj_b")
    f = np.float32
    parts = {
        "in_w": a("attn_in_proj_w").T, "gate": a("ffn_gate_w"),
        "xp_dt": rows(xp[:DR].T), "xp_bc": rows(bc), "out_w": rows(a("attn_out_proj_w").T),
        "write_w": a("attn_proj_write_w").T, "read_w": a("attn_proj_read_w").T,
        "norm1": a("attn_norm1_w")[:, None], "norm2": a("attn_norm2_w")[:, None],
        "in_b": rows(a("attn_in_proj_b")[:, None]), "conv_w": rows(a("attn_conv_w")[:, 0, :]),
        "conv_b": rows(a("attn_conv_b")[:, None]), "dt_b": rows(a("attn_dt_proj_b")[:, None]),
        "A_log": rows(a("attn_A_log")), "D_ssm": rows(a("attn_D_ssm")[:, None]), "out_b": ob[:, None],
        "decay": np.broadcast_to(a("attn_decay").reshape(1, 1), (P, 1)),
        "dt_w": fill(a("attn_dt_proj_w").T), "out_b_row": fill(ob[None, :]),
        "ident": np.eye(P, dtype=f), "dist": np.maximum(t - 1 - s, 0).astype(f), "causal": (t > s).astype(f),
        "iota": np.broadcast_to(np.arange(E, dtype=f), (P, E)), "ones_row": fill(np.ones((1, P), f)),
    }
    pack = np.ascontiguousarray(np.concatenate([parts[n] for n, _ in PACK], 1))
    sel = np.zeros((4 * DS, 2 * DS, P), f)
    sel[np.arange(4 * DS), np.arange(4 * DS) % (2 * DS), :] = 1.0
    arrays = {
        "x_dram": np.ascontiguousarray(a("attn_x").reshape(BATCH * T, D)), "pack_dram": pack,
        "sel_dram": sel.reshape(4 * DS, -1), "w1_dram": np.ascontiguousarray(a("ffn_w1s")),
        "w2_dram": np.ascontiguousarray(a("ffn_w2s")),
    }
    nc = bacc.Bacc("TRN2", target_bir_lowering=False, num_devices=1)
    args = [nc.dram_tensor(n, v.shape, mybir.dt.float32, kind="ExternalInput").ap() for n, v in arrays.items()]
    out = nc.dram_tensor("out_dram", (BATCH * T, D), mybir.dt.float32, kind="ExternalOutput").ap()
    moe_mamba_kernel(nc, *args, out)
    r = run_bass_kernel_spmd(nc, [arrays], core_ids=[0])
    return r.results[0]["out_dram"].reshape(BATCH, T, D)
```

```python
import concourse.bass as bass
from concourse import mybir
from contextlib import ExitStack

P = 128
BATCH, T, D = 16, 256, 128
E, HID = 8, 512
DI, DS, DR, DC = 256, 16, 64, 4
SEQ = 2
TOK = SEQ * T
TILES = TOK // P
GROUPS = BATCH // SEQ
HC = HID // P
HALVES = DI // P
PAD = DC - 1
EPS = 1e-5

PACK = [("gate", E), ("xp_dt", HALVES * DR), ("xp_bc", HALVES * 4 * DS),
        ("out_w", HALVES * D), ("write_w", D), ("read_w", D), ("norm1", 1), ("norm2", 1),
        ("in_b", 2 * HALVES), ("conv_b", HALVES), ("conv_w", HALVES * DC), ("dt_b", HALVES),
        ("A_log", HALVES * DS), ("D_ssm", HALVES), ("out_b", 1), ("decay", 1), ("dt_w", DI),
        ("out_b_row", D), ("ident", P), ("dist", T), ("causal", T), ("iota", E), ("tap_b", DI), ("ones_row", P),
        ("outside", PAD)]

DP = 2
NP = DS // DP
SPREAD = [t for j in range(NP + 1) for t in ((0, j), (1, j - 1)) if 0 <= t[1] < NP]
NG = 3
RING = 3
SHIFT = (0, 1, 2, 0)
PAIR = 4 * HC
PIECES = E // 2 * PAIR

ORDER = {
    "tensor": (
        "t0 t1 fturn in t2 fgate p2 t3 p2 t4 p5 t5 p2 t6 t7 xp p1 dt p2 t8 p1 t9 p2 t10 p3 m1 t11 p2 t12 "
        "t13 p4 m2 p3 t14 m3 t15 p1 m4 p1",
        "p2 t0 t1 t2 p5 out p6 turn t3 p1 t4 t5 in p2 t6 t7 p2 t8 t9 xp p1 t10 p2 t11 p1 t12 p1 dt p4 t13 "
        "t14 p6 t15",
        "t0 fturn t1 fgate p1 t2 p1 t3 out p4 t4 p5 turn t5 p2 t6 in t7 t8 p1 t9 p3 t10 xp p1 t11 p2 t12 p2 "
        "t13 p2 dt t14 t15",
        "p5 t0 p1 turng t1 p3 in t2 t3 t4 p8 t5 t6 xp p4 t7 t8 dt m1 p1 t9 t10 p3 t11 p1 m2 p2 t12 p2 t13 "
        "t14 p2 m3 p5 t15 p3 m4"),
    "scalar": (
        "d0 fhigh d1 d2 r xm F0 ftanh F1 d3 d4 proj d5 sp F2 F3 oT d6 v d7 rT",
        "d0 d1 F4 F5 d2 turned d3 d4 d5 d6 r xm F6 proj F7 d7 sp",
        "fhigh d0 d1 d2 F0 F1 ftanh d3 turned d4 d5 d6 d7 r xm F2 proj F3 sp",
        "turned d0 d1 d2 F4 r xm F5 d3 proj d4 d5 d6 sp oT F6 v F7 rT d7"),
    "vector": (
        "gate flow b0 flog ftop b1 s0 s1 g0 b2 g1 b3 s2 s3 fweights g2 b4 low f0 s4 f1 g3 b5 g4 s5 b6 g5 b7 "
        "delta mask s6 g6 s7 g7 xb f2",
        "f3 fstats gate b0 b1 s0 xsum s1 un g0 b2 g1 s2 f4 b3 fnorm s3 g2 f5 b4 g3 b5 s4 s5 g4 b6 g5 s6 b7 "
        "low s7 g6 f6 f7 g7 delta",
        "flow b0 flog gate s0 b1 g0 xsum ftop b2 un s1 s2 g1 b3 lx fweights s3 g2 b4 f0 g3 f1 s4 b5 g4 s5 "
        "b6 g5 b7 s6 s7 ln low unx g6 delta g7",
        "f2 b0 b1 f3 s0 gate g0 b2 s1 s2 fstats g1 b3 low g2 s3 b4 g3 f4 s4 f5 b5 g4 b6 delta mask s5 s6 g5 "
        "b7 g6 s7 g7 f6 fnorm f7 xb"),
    "gpsimd": (
        "a1 a2 a3 a4 a5 a6 a7",
        "rms rs froot a1 a2 a3 a4 a5 a6 a7",
        "rms a1 a2 rs lnx rmsx a3 a4 a5 a6 a7",
        "a1 a2 a3 a4 froot a5 a6 a7"),
}


def steps(engine, i):
    for word in ORDER[engine][i].split():
        name = word.rstrip("0123456789")
        yield name, int(word[len(name):] or 0)


def pieces_in(i):
    return sum(n for name, n in steps("tensor", i) if name == "p")


COL, WIDTH = {}, 0
for _name, _w in PACK:
    COL[_name] = (WIDTH, WIDTH + _w)
    WIDTH += _w


def moe_mamba_kernel(nc, x, pack, early, sel, w1, w2, out):
    fp32, fp32r, u32 = mybir.dt.float32, mybir.dt.float32r, mybir.dt.uint32
    ALU, ACT = mybir.AluOpType, mybir.ActivationFunctionType

    ctx = ExitStack()
    with ctx:
        def sb(name, shape, dt=fp32):
            return ctx.enter_context(nc.sbuf_tensor(name, shape, dt))

        prm = sb("prm", [P, WIDTH])
        raw = sb("raw", [P, E * HID])
        w1h = sb("w1h", [P, E, HID], fp32r)
        w1l = sb("w1l", [P, E, HID], fp32r)
        w2s = sb("w2s", [P, E, HC, D])
        selr = sb("selr", [4 * DS, 2 * DS, P], fp32r)
        ghl = sb("ghl", [P, 2, E], fp32r)
        inx = sb("inx", [P, 2, DC, DI])
        inz = sb("inz", [P, 2, DI])
        tapw = sb("tapw", [P, HALVES])
        convb = sb("convb", [P, HALVES])
        A = sb("A", [P, HALVES, DS])
        lgam = sb("lgam", [P, 4])
        powh = sb("powh", [P, TILES])
        epst = sb("epst", [P, TILES])

        def par(name):
            a, b = COL[name]
            return prm[:, a:b]

        MT = prm[:, COL["dist"][0]:COL["dist"][0] + T + P]

        xin = sb("xin", [P, TILES, D])
        stats = sb("stats", [P, TILES, 6])
        mv = sb("mv", [P, TILES, 2])
        rstd = sb("rstd", [P, TILES])
        xn = sb("xn", [P, TILES, D])
        xh = sb("xh", [P, TOK], fp32r)
        xl = sb("xl", [P, TOK], fp32r)
        lg = sb("lg", [P, TILES, E])
        m8 = sb("m8", [P, TILES, 8])
        ix = sb("ix", [P, TILES, 8], u32)
        ixf = sb("ixf", [P, TILES, 8])
        gap = sb("gap", [P, TILES])
        th = sb("th", [P, TILES])
        c01 = sb("c01", [P, 2, TILES])
        hit = sb("hit", [P, 2, TILES, E])
        comb = sb("comb", [P, TILES, E])
        hT = [raw[:, i * HC * TOK:(i + 1) * HC * TOK].rearrange("p (c t) -> p c t", c=HC)
              for i in range(2)]
        xa = sb("xa", [P, TILES, D])
        xb = sb("xb", [P, TILES, D])
        ob = sb("ob", [P, TILES, D])

        xam = sb("xam", [P, TILES, D])
        statm = sb("statm", [P, TILES, 6])
        mvm = sb("mvm", [P, TILES, 2])
        rstdm = sb("rstdm", [P, TILES])
        statr = sb("statr", [P, TILES, 6])
        mvr = sb("mvr", [P, TILES, 2])
        rstdr = sb("rstdr", [P, TILES])
        varr = sb("varr", [P, TILES])
        vr = sb("vr", [P, TILES])
        ln = sb("ln", [P, TILES, D])
        x1 = sb("x1", [P, TILES, D])
        rs = sb("rs", [P, TILES, D])
        un = sb("un", [P, TILES, D])
        uT = sb("uT", [P, SEQ, PAD + T])
        xm = [sb(f"xm{b}", [P, HALVES, T]) for b in range(SEQ)]
        sres = [sb(f"sres{b}", [P, HALVES, T]) for b in range(SEQ)]
        bcr = [sb(f"bcr{b}", [4 * DS, T], fp32r) for b in range(SEQ)]
        delta = [sb(f"delta{b}", [P, HALVES, T]) for b in range(SEQ)]
        du = [sb(f"du{b}", [P, HALVES, T]) for b in range(SEQ)]
        acc = [sb(f"acc{b}", [P, DP, HALVES, T]) for b in range(SEQ)]
        dtT = sb("dtT", [DR, T])
        z = sb("z", [P, HALVES, T])
        ez = sb("ez", [P, HALVES, T])
        yg = sb("yg", [P, HALVES, T])
        dA = [sb(f"dA{i}", [P, DP, HALVES, T]) for i in range(4)]
        dbu = [sb(f"dbu{i}", [P, DP, HALVES, T]) for i in range(2)]
        hs = [sb(f"hs{i}", [P, DP, HALVES, T]) for i in range(2)]
        G = [sb(f"G{i}", [P, DP, HALVES, T]) for i in range(NG)]
        oT = sb("oT", [P, 1 + T])
        vt = sb("vt", [P, T // P, D])
        rT = vt[:, :, :].rearrange("p j d -> p (j d)")
        SM = sb("SM", [P, T + P])

        flat_in = [t[:, :, :, :].rearrange("p d h t -> p (d h t)") for t in (dbu[0], dA[0], hs[0], hs[1], G[0], G[1])]
        win, taps, sel_in = flat_in[0], flat_in[1], [t[0:4 * DS, :] for t in flat_in[2:]]
        N_SEL = DP * HALVES * T

        bank = [ctx.enter_context(nc.psum_tensor(n, [P, 512], fp32))
                for n in ("b_out", "b_h0", "b_h1", "b_w0", "b_w1", "b_r0", "b_r1", "b_r2")]
        OUT, H, W, R = bank[0], bank[1:3], bank[3:5], bank[5:8]
        EOUT = (OUT, H[1])

        def sem(name):
            return ctx.enter_context(nc.semaphore(name))

        s_pack, s_w1, s_w2, s_sel, s_early, s_gate = (
            sem("s_pack"), sem("s_w1"), sem("s_w2"), sem("s_sel"), sem("s_early"), sem("s_gate"))
        s_raw_read, s_lg, s_Aexp, s_set_dve, s_set_act, s_exponent = (
            sem("s_raw_read"), sem("s_lg"), sem("s_Aexp"), sem("s_set_dve"), sem("s_set_act"),
            sem("s_exponent"))
        s_xin, s_store = sem("s_xin"), sem("s_store")
        f_stats, f_rstd, f_xn, f_xnT, f_split, f_logits, f_lread, f_gap, f_th, f_xh = (
            sem("f_stats"), sem("f_rstd"), sem("f_xn"), sem("f_xnT"), sem("f_split"),
            sem("f_logits"), sem("f_lread"), sem("f_gap"), sem("f_th"), sem("f_xh"))
        f_hmm, f_hact, f_ymm, f_yacc = sem("f_hmm"), sem("f_hact"), sem("f_ymm"), sem("f_yacc")
        g_stats, g_rstd, g_xam, g_ln, g_x1, g_rs, g_xb = (
            sem("g_stats"), sem("g_rstd"), sem("g_xam"), sem("g_ln"), sem("g_x1"), sem("g_rs"), sem("g_xb"))
        g_oTmm, g_oT, g_vmm, g_v, g_smm, g_sm, g_rmm, g_r = (
            sem("g_oTmm"), sem("g_oT"), sem("g_vmm"), sem("g_v"), sem("g_smm"), sem("g_sm"),
            sem("g_rmm"), sem("g_r"))
        q_stats, q_rstd, q_u, q_uTmm, q_uT, q_xz, q_xm, q_res = (
            sem("q_stats"), sem("q_rstd"), sem("q_u"), sem("q_uTmm"), sem("q_uT"), sem("q_xz"),
            sem("q_xm"), sem("q_res"))
        q_xmm, q_bc, q_dt, q_zmm, q_sp, q_delta = (
            sem("q_xmm"), sem("q_bc"), sem("q_dt"), sem("q_zmm"), sem("q_sp"), sem("q_delta"))
        q_dA, q_B, q_C, q_dbu, q_scan, q_G, q_gs, q_yg, q_omm, q_bch = (
            sem("q_dA"), sem("q_B"), sem("q_C"), sem("q_dbu"), sem("q_scan"), sem("q_G"),
            sem("q_gs"), sem("q_yg"), sem("q_omm"), sem("q_bch"))

        def piece(k):
            pair, i = divmod(k, PAIR)
            down, i = divmod(i, 2 * HC)
            return bool(down), 2 * pair + i // HC, i % HC

        def wait(eng, s, value):
            if not isinstance(value, int) or value > 0:
                eng.wait_ge(s, value)

        def both(t):
            return t[:, :].rearrange("p (k t) -> p k t", k=2)

        def turn_no(g, i):
            return 3 * g + max(i - 1, 0)

        def first(g):
            return g if g < 2 else 2 * g - 2

        def second(g):
            return 2 * g + 3 if g < GROUPS - 2 else g + GROUPS

        block = ctx.enter_context(nc.Block())

        @block.sync
        def _(sp):
            xt = x.rearrange("(g j p) d -> g p j d", p=P, j=TILES)
            ot = out.rearrange("(g j p) d -> g p j d", p=P, j=TILES)
            sp.dma_start(prm[:, :], pack).then_inc(s_pack, 16)
            sp.dma_start(xin[:, :, :], xt[0]).then_inc(s_xin, 16)
            sp.dma_start(raw[:, :].rearrange("p (e h) -> p e h", e=E),
                         w1.rearrange("e d h -> d e h")).then_inc(s_w1, 16)
            sp.dma_start(win[:, 0:3 * DI], early[:, 0:3 * DI]).then_inc(s_early, 16)
            sp.dma_start(taps, early[:, 3 * DI:]).then_inc(s_early, 16)
            sp.dma_start(w2s[:, :, :, :].rearrange("p e c d -> p (e c) d"),
                         w2.rearrange("e (c p) d -> p (e c) d", p=P)).then_inc(s_w2, 16)
            for i, b in enumerate(sel_in):
                sp.dma_start(b, sel[:, i * N_SEL:(i + 1) * N_SEL]).then_inc(s_sel, 16)

            def store(g):
                sp.wait_ge(f_yacc, (second(g) + 1) * E)
                sp.dma_start(ot[g], ob[:, :, :]).then_inc(s_store, 16)

            for g in range(GROUPS):
                if g + 1 < GROUPS:
                    sp.wait_ge(f_yacc, first(g) * E + 1)
                    sp.dma_start(xin[:, :, :], xt[g + 1]).then_inc(s_xin, 16)
                if g >= 2:
                    store(g - 2)
            store(GROUPS - 2)
            store(GROUPS - 1)
            sp.wait_ge(s_store, 16 * GROUPS)

        @block.tensor
        def _(pe):
            mm = nc.tensor.matmul
            ident = par("ident")

            def ffn_turn(n):
                pe.wait_ge(f_xn, n + 1)
                wait(pe, f_yacc, n * E)
                for j in range(TILES):
                    last = nc.tensor.transpose(OUT[:, j * P:(j + 1) * P], xn[:, j, :], ident)
                last.then_inc(f_xnT, 1)

            def ffn_gate(n):
                pe.wait_ge(f_split, n + 1)
                wait(pe, f_hact, n * E * HC)
                for j in range(TILES):
                    t = slice(j * P, (j + 1) * P)
                    o = H[0][:, 2 * j * E:2 * (j + 1) * E]
                    mm(o, xh[:, t], ghl[:, :, :].rearrange("p k e -> p (k e)"), start=True, stop=False)
                    last = mm(o, xl[:, t], ghl[:, :, :].rearrange("p k e -> p (k e)"), start=False, stop=True)
                last.then_inc(f_logits, 1)

            def ffn_up(n, e, c):
                i = e * HC + c
                if i == 0:
                    pe.wait_ge(f_lread, n + 1)
                else:
                    wait(pe, f_hact, n * E * HC + i - 1)
                if e % 2 == 0 and e > 0 and c == 1:
                    pe.wait_ge(f_yacc, n * E + e)
                w = slice(c * P, (c + 1) * P)
                h = H[i % 2][:, :]
                mm(h, w1h[:, e, w], xh[:, :], start=True, stop=False)
                mm(h, w1h[:, e, w], xl[:, :], start=False, stop=False)
                mm(h, w1l[:, e, w], xh[:, :], start=False, stop=True).then_inc(f_hmm, 1)

            def ffn_down(n, e, j):
                if j == 0:
                    pe.wait_ge(f_hact, (n * E + e + 1) * HC)
                    wait(pe, f_yacc, n * E + e - 1)
                for c in range(HC):
                    last = mm(EOUT[e % 2][:, j * D:(j + 1) * D], hT[e % 2][:, c, j * P:(j + 1) * P],
                              w2s[:, e, c, :], start=c == 0, stop=c == HC - 1)
                if j == TILES - 1:
                    last.then_inc(f_ymm, 1)

            def turn(g, i):
                tiles = range(TILES) if i == 0 else range(T // P)
                pe.wait_ge(q_u, turn_no(g, i) + 1)
                wait(pe, q_sp, 4 * g + i)
                for j in tiles:
                    last = nc.tensor.transpose(W[1][:, j * P:(j + 1) * P],
                                               un[:, (i % 2 * (T // P) if i else 0) + j, :], ident)
                last.then_inc(q_uTmm, 1)

            def in_proj(g, i):
                q, b = 4 * g + i, i % 2
                pe.wait_ge(q_uT, turn_no(g, i) + 1)
                if i == 1:
                    pe.wait_ge(q_sp, q)
                    wait(pe, g_xb, 2 * g - 1)
                m = i // 2
                for k in range(HALVES):
                    o, ch = W[0][:, k * T:(k + 1) * T], slice(k * P, (k + 1) * P)
                    for r in range(DC):
                        last = mm(o, inx[:, m, r, ch], uT[:, b, PAD - r:PAD - r + T], start=r == 0, stop=r == PAD)
                        if r == 0:
                            mm(W[0][:, k * T:k * T + PAD], par("tap_b")[0:DC, ch], par("outside")[0:DC, :],
                               start=False, stop=False)
                last.then_inc(q_xz, 1)
                for k in range(HALVES):
                    last = mm(W[1][:, k * T:(k + 1) * T], inz[:, m, k * P:(k + 1) * P], uT[:, b, PAD:],
                              start=True, stop=True)
                last.then_inc(q_xz, 1)

            def x_proj(g, i):
                q, b = 4 * g + i, i % 2
                pe.wait_ge(q_xm, 2 * q + 2)
                for o, w in ((W[0][0:DR, 0:T], "xp_dt"), (W[0][0:4 * DS, T:], "xp_bc")):
                    wd = par(w)
                    n = o.shape[0]
                    for k in range(HALVES):
                        last = mm(o, wd[:, k * n:(k + 1) * n], xm[b][:, k, :], start=k == 0, stop=k == HALVES - 1)
                last.then_inc(q_xmm, 1)

            def dt_proj(g, i):
                q = 4 * g + i
                pe.wait_ge(q_dt, q + 1)
                for k in range(HALVES):
                    last = mm(W[1][:, k * T:(k + 1) * T], par("dt_w")[0:DR, k * P:(k + 1) * P], dtT[:, :],
                              start=True, stop=True)
                last.then_inc(q_zmm, 1)

            def spread(g, i, t):
                q, b = 4 * g + i, i % 2
                if t == 0:
                    pe.wait_ge(q_bc, q + 1)
                ring = lambda i, t: (t + SHIFT[i]) % RING
                if t >= RING:
                    kind, j = SPREAD[t - RING]
                    pe.wait_ge(q_G if kind else q_dbu, q * NP + j + 1)
                else:
                    kind, j = next(SPREAD[o] for o in range(2 * NP - RING, 2 * NP)
                                   if ring((i - 1) % 4, o) == ring(i, t))
                    if not isinstance(g, int) or q > 0:
                        pe.wait_ge(q_G if kind else q_dbu, q * NP - NP + j + 1)
                kind, j = SPREAD[t]
                for d in range(DP):
                    last = mm(R[ring(i, t)][:, d * T:(d + 1) * T], selr[:, kind * DS + DP * j + d, :], bcr[b][:, :],
                              start=True, stop=True)
                last.then_inc(q_C if kind else q_B, 1)

            def out_proj(o, j, stop):
                for k in range(HALVES):
                    mm(o, yg[:, k, j * P:(j + 1) * P], par("out_w")[:, k * D:(k + 1) * D], start=k == 0, stop=False)
                return mm(o, par("ones_row")[0:1, :], par("out_b_row")[0:1, :], start=False, stop=stop)

            def first_out(g, i):
                q = 4 * g + i
                pe.wait_ge(q_yg, q + 1)
                for j in range(T // P):
                    last = out_proj(W[0][:, j * D:(j + 1) * D], j, True)
                last.then_inc(q_omm, 1)

            def memory_1(g, b, head):
                q = 4 * g + 2 + b
                pe.wait_ge(q_yg, q + 1)
                if head:
                    pe.wait_ge(q_bc, q + 3)
                for k in range(HALVES):
                    last = mm(W[0][:, 0:T], par("out_w")[:, k * D:(k + 1) * D], yg[:, k, :],
                              start=k == 0, stop=k == HALVES - 1)
                last.then_inc(g_oTmm, 1)

            def memory_2(g, b):
                pe.wait_ge(g_oT, 2 * g + b + 1)
                for j in range(T // P):
                    last = mm(W[0][:, T + j * D:T + (j + 1) * D], oT[:, 1 + j * P:1 + (j + 1) * P], par("write_w"),
                              start=True, stop=True)
                last.then_inc(g_vmm, 1)
                mm(W[1][:, 0:T], oT[:, 0:P], oT[:, 1:1 + T], start=True, stop=True)
                mm(W[1][:, T:T + P], oT[:, P:T], oT[:, 1 + P:1 + T], start=True, stop=True).then_inc(g_smm, 1)

            def memory_3(g, b):
                pe.wait_ge(g_v, 2 * g + b + 1)
                pe.wait_ge(g_sm, 2 * g + b + 1)
                mm(W[0][:, 0:P], vt[:, 0, :], SM[:, 0:P], start=True, stop=True)
                mm(W[0][:, P:T], vt[:, 0, :], SM[:, P:T], start=True, stop=False)
                mm(W[0][:, P:T], vt[:, 1, :], SM[:, T:T + P], start=False, stop=True).then_inc(g_rmm, 1)

            def memory_4(g, b):
                pe.wait_ge(g_r, 2 * g + b + 1)
                for j in range(T // P):
                    o = W[1][:, j * D:(j + 1) * D]
                    out_proj(o, j, False)
                    last = mm(o, rT[:, j * P:(j + 1) * P], par("read_w"), start=False, stop=True)
                last.then_inc(q_omm, 1)

            def slot(g, i, tail, head, n, nx):
                k = pieces_in(i - 1) if i % 2 else 0
                for name, num in steps("tensor", i):
                    if name == "t":
                        spread(g, i, num)
                    elif name == "p":
                        if n is not None:
                            for x in range(k, k + num):
                                down, e, part = piece(x)
                                (ffn_down if down else ffn_up)(n, e, part)
                        k += num
                    elif name in ("fturn", "fgate"):
                        if n is not None:
                            (ffn_turn if name == "fturn" else ffn_gate)(n)
                    elif name == "turng":
                        if head:
                            turn(head[0], 0)
                    elif name in ("in", "xp", "dt", "turn"):
                        if head:
                            {"in": in_proj, "xp": x_proj, "dt": dt_proj, "turn": turn}[name](*head)
                    elif tail:
                        if name == "out":
                            first_out(*tail)
                        elif num == 1:
                            memory_1(tail[0], tail[1] - 2, head)
                        else:
                            (memory_2, memory_3, memory_4)[num - 2](tail[0], tail[1] - 2)
                assert i % 2 == 0 or k == PIECES

            def ffn_pieces(n):
                for x in range(PIECES):
                    down, e, part = piece(x)
                    (ffn_down if down else ffn_up)(n, e, part)

            def alone(n):
                ffn_turn(n)
                ffn_gate(n)
                ffn_pieces(n)

            def start():
                ffn_turn(first(0))
                pe.wait_ge(s_gate, 1)
                ffn_gate(first(0))
                pe.wait_ge(s_raw_read, 1)
                pe.wait_ge(s_w2, 16)
                ffn_pieces(first(0))
                pe.wait_ge(s_set_dve, 1)
                turn(0, 0)
                in_proj(0, 0)
                x_proj(0, 0)
                dt_proj(0, 0)

            def finish():
                tail = (GROUPS - 1, 1)
                memory_1(*tail, None)
                memory_2(*tail)
                memory_3(*tail)
                memory_4(*tail)
                alone(second(GROUPS - 1))

            pe.wait_ge(s_pack, 16)
            def run(g, n1, n2, n3, is_last):
                for i in range(4):
                    tail = (g, i - 1) if i else None if isinstance(g, int) and g == 0 else (g - 1, 3)
                    head = (g, i + 1) if i < 3 else None if is_last else (g + 1, 0)
                    slot(g, i, tail, head, (n1, n2)[i // 2], (n2, n3)[i // 2])

            start()
            run(0, first(1), None, first(2), False)
            with pe.Fori(1, GROUPS - 2) as g:
                run(g, g * 2, g * 2 + 1, g * 2 + 2, False)
            run(GROUPS - 2, first(GROUPS - 1), second(GROUPS - 3), None, False)
            run(GROUPS - 1, None, second(GROUPS - 2), None, True)
            finish()

        @block.scalar
        def _(act):
            do = nc.scalar.activation

            act.wait_ge(s_pack, 16)
            do(lgam[:, 0:1], par("decay"), ACT.Abs)
            act.drain()
            do(lgam[:, 1:2], lgam[:, 0:1], ACT.Exp, scale=-1.0)
            act.drain()
            do(lgam[:, 2:3], lgam[:, 1:2], ACT.Ln, bias=1.0).then_inc(s_lg, 1)
            do(A[:, :, :], par("A_log").rearrange("p (h s) -> p h s", s=DS), ACT.Exp).then_inc(s_Aexp, 1)
            act.wait_ge(s_exponent, 1)
            do(MT[:, 0:T], par("dist"), ACT.Exp, scale=lgam[:, 3:4]).then_inc(s_set_act, 1)

            def ffn_high(n):
                act.wait_ge(f_xnT, n + 1)
                wait(act, f_hmm, n * E * HC)
                do(xh[:, :], OUT[:, :], ACT.Copy).then_inc(f_xh, 1)

            def ffn_gate(n):
                act.wait_ge(f_gap, n + 1)
                do(th[:, :], gap[:, :], ACT.Tanh, scale=0.5).then_inc(f_th, 1)

            def ffn_silu(n, e):
                for c in range(HC):
                    i = e * HC + c
                    if c == 0:
                        wait(act, f_ymm, n * E + e - 1)
                    act.wait_ge(f_hmm, n * E * HC + i + 1)
                    do(hT[e % 2][:, c, :], H[i % 2][:, :], ACT.Silu).then_inc(f_hact, 1)

            def turned(g, i):
                act.wait_ge(q_uTmm, turn_no(g, i) + 1)
                if i == 0:
                    wait(act, q_xz, 8 * g)
                    do(uT[:, :, PAD:], both(W[1]), ACT.Copy).then_inc(q_uT, 1)
                else:
                    wait(act, q_xz, 2 * (4 * g + i - 1))
                    b = i % 2
                    do(uT[:, b, PAD:], W[1][:, 0:T], ACT.Copy).then_inc(q_uT, 1)

            def gate_input(g, i):
                q, b = 4 * g + i, i % 2
                wait(act, q_yg, q - 1)
                act.wait_ge(q_xz, 2 * q + 2)
                for k in range(HALVES):
                    do(sres[b][:, k, :], W[1][:, k * T:(k + 1) * T], ACT.Silu,
                       bias=par("in_b")[:, 2 + k:3 + k]).then_inc(q_res, 1)

            def conv_silu(g, i):
                q, b = 4 * g + i, i % 2
                act.wait_ge(q_xz, 2 * q + 1)
                wait(act, q_yg, q - 1)
                for k in range(HALVES):
                    do(xm[b][:, k, :], W[0][:, k * T:(k + 1) * T], ACT.Silu, bias=convb[:, k:k + 1]).then_inc(q_xm, 1)

            def projections(g, i):
                q, b = 4 * g + i, i % 2
                act.wait_ge(q_xmm, q + 1)
                wait(act, q_zmm, q)
                do(dtT[:, :], W[0][0:DR, 0:T], ACT.Copy).then_inc(q_dt, 1)
                wait(act, q_C, (q - 1) * NP)
                do(bcr[b][:, :], W[0][0:4 * DS, T:], ACT.Copy).then_inc(q_bch, 1)

            def softplus(g, i):
                q = 4 * g + i
                act.wait_ge(q_zmm, q + 1)
                wait(act, q_delta, q)
                for o, f in ((ez, ACT.Abs), (z, ACT.Identity)):
                    for k in range(HALVES):
                        do(o[:, k, :], W[1][:, k * T:(k + 1) * T], f, bias=par("dt_b")[:, k:k + 1])
                act.drain()
                do(ez[:, :, :], ez[:, :, :], ACT.Exp, scale=-1.0)
                act.drain()
                do(ez[:, :, :], ez[:, :, :], ACT.Ln, bias=1.0).then_inc(q_sp, 1)

            def decays(g, i, j):
                q, b = 4 * g + i, i % 2
                if j == 0:
                    act.wait_ge(q_delta, q + 1)
                wait(act, q_scan, q * NP + j - 3)
                for d in range(DP):
                    s = DP * j + d
                    for k in range(HALVES):
                        last = do(dA[j % 4][:, d, k, 1:], delta[b][:, k, 1:], ACT.Exp, scale=A[:, k, s:s + 1])
                last.then_inc(q_dA, 1)

            def memory_out(g, b):
                act.wait_ge(g_oTmm, 2 * g + b + 1)
                do(oT[:, 1:], W[0][:, 0:T], ACT.Identity, bias=par("out_b")).then_inc(g_oT, 1)

            def memory_v(g, b):
                act.wait_ge(g_vmm, 2 * g + b + 1)
                do(vt[:, :, :], W[0][:, T:].rearrange("p (j d) -> p j d", d=D), ACT.Copy).then_inc(g_v, 1)

            def memory_reads(g, b):
                act.wait_ge(g_rmm, 2 * g + b + 1)
                do(rT[:, :], W[0][:, 0:T], ACT.Copy).then_inc(g_r, 1)

            def slot(g, i, tail, head, n, nx):
                for name, num in steps("scalar", i):
                    if name == "d":
                        decays(g, i, num)
                    elif name == "F":
                        if n is not None:
                            ffn_silu(n, num)
                    elif name == "ftanh":
                        if n is not None:
                            ffn_gate(n)
                    elif name == "fhigh":
                        if n is not None:
                            ffn_high(n)
                    elif name in ("oT", "v", "rT"):
                        if tail:
                            {"oT": memory_out, "v": memory_v, "rT": memory_reads}[name](tail[0], tail[1] - 2)
                    elif head:
                        {"turned": turned, "r": gate_input,
                         "xm": conv_silu, "proj": projections, "sp": softplus}[name](*head)

            def alone(n):
                ffn_high(n)
                for e in range(E):
                    ffn_silu(n, e)
                    if e == 0:
                        ffn_gate(n)

            def start():
                ffn_high(first(0))
                act.wait_ge(s_raw_read, 1)
                for e in range(E):
                    ffn_silu(first(0), e)
                    if e == 0:
                        ffn_gate(first(0))
                act.wait_ge(s_set_dve, 1)
                turned(0, 0)
                gate_input(0, 0)
                conv_silu(0, 0)
                projections(0, 0)
                softplus(0, 0)

            def finish():
                tail = (GROUPS - 1, 1)
                memory_out(*tail)
                memory_v(*tail)
                memory_reads(*tail)
                alone(second(GROUPS - 1))

            def run(g, n1, n2, n3, is_last):
                for i in range(4):
                    tail = (g, i - 1) if i else None if isinstance(g, int) and g == 0 else (g - 1, 3)
                    head = (g, i + 1) if i < 3 else None if is_last else (g + 1, 0)
                    slot(g, i, tail, head, (n1, n2)[i // 2], (n2, n3)[i // 2])

            start()
            run(0, first(1), None, first(2), False)
            with act.Fori(1, GROUPS - 2) as g:
                run(g, g * 2, g * 2 + 1, g * 2 + 2, False)
            run(GROUPS - 2, first(GROUPS - 1), second(GROUPS - 3), None, False)
            run(GROUPS - 1, None, second(GROUPS - 2), None, True)
            finish()

        @block.vector
        def _(dve):
            V = nc.vector

            def norm_stats(src, st, agg, tiles=range(TILES)):
                for j in tiles:
                    V.bn_stats(st[:, j, :], src[:, j, :])
                dve.drain()
                for j in tiles:
                    last = V.bn_aggr(agg[:, j, :], st[:, j, :])
                return last

            def split_gate():
                dve.wait_ge(s_pack, 16)
                V.tensor_copy(ghl[:, 0, :], par("gate"))
                dve.drain()
                V.tensor_tensor(ghl[:, 1, :], par("gate"), ghl[:, 0, :].bitcast(fp32), ALU.subtract).then_inc(s_gate, 1)

            def split_w1():
                dve.wait_ge(s_w1, 16)
                rv = raw[:, :].rearrange("p (e h) -> p e h", e=E)
                V.tensor_copy(w1h[:, :, :], rv)
                dve.drain()
                V.tensor_tensor(w1l[:, :, :], rv, w1h[:, :, :].bitcast(fp32), ALU.subtract).then_inc(s_raw_read, 1)

            def exponent():
                dve.wait_ge(s_lg, 1)
                V.tensor_scalar(lgam[:, 0:1], par("decay"), 0.0, None, ALU.min)
                dve.drain()
                V.tensor_tensor(lgam[:, 3:4], lgam[:, 0:1], lgam[:, 2:3], ALU.subtract).then_inc(s_exponent, 1)

            def mixer_weights():
                dve.wait_ge(s_early, 32)
                for m, nw in enumerate(("norm1", "norm2")):
                    V.tensor_scalar(inz[:, m, :], win[:, DI:2 * DI], par(nw), None, ALU.mult)
                    for r in range(DC):
                        V.scalar_tensor_tensor(out=inx[:, m, r, :], in0=win[:, 0:DI], scalar=par(nw),
                                               in1=taps[:, r * DI:(r + 1) * DI], op0=ALU.mult, op1=ALU.mult)
                V.tensor_tensor(par("tap_b"), par("tap_b"), win[:, 2 * DI:3 * DI], ALU.mult)
                V.tensor_scalar(par("read_w"), par("read_w"), 0.1, None, ALU.mult)
                V.tensor_reduce(tapw[:, :], par("conv_w").rearrange("p (k j) -> p k j", j=DC),
                                mybir.AxisListType.X, ALU.add)
                dve.drain()
                V.tensor_tensor(convb[:, :], tapw[:, :], par("in_b")[:, 0:HALVES], ALU.mult)
                dve.drain()
                V.tensor_tensor(convb[:, :], convb[:, :], par("conv_b"), ALU.add)
                dve.wait_ge(s_sel, 16 * len(sel_in))
                for i, b in enumerate(sel_in):
                    rows = N_SEL // P
                    V.tensor_copy(selr[:, i * rows:(i + 1) * rows, :], b.rearrange("p (i m) -> p i m", m=P))
                dve.wait_ge(s_Aexp, 1)
                V.tensor_scalar(A[:, :, :], A[:, :, :], -1.0, None, ALU.mult)
                dve.wait_ge(s_set_act, 1)
                V.tensor_tensor(MT[:, 0:T], MT[:, 0:T], par("causal"), ALU.mult)
                dve.drain()
                V.tensor_copy(MT[:, T:T + P], MT[:, 0:P])
                V.memset(oT[:, 0:1], 0.0)
                V.memset(uT[:, :, 0:PAD], 0.0)
                for i in range(4):
                    V.memset(dA[i][:, :, :, 0:1], 0.0)
                dve.drain()
                V.memset(gap[:, :], 0.0).then_inc(s_set_dve, 1)

            def ffn_stats(f):
                n, src, dst, g, is_first = f
                if is_first:
                    dve.wait_ge(s_xin, g * 16 + 16)
                else:
                    dve.wait_ge(g_xb, SEQ * (g + 1))
                norm_stats(src, stats, mv).then_inc(f_stats, 1)

            def ffn_norm(f):
                n, src, dst, g, is_first = f
                dve.wait_ge(f_rstd, n + 1)
                wait(dve, f_xnT, n)
                for j in range(TILES):
                    last = V.tensor_scalar(xn[:, j, :], src[:, j, :], mv[:, j, 0:1], rstd[:, j:j + 1],
                                           ALU.subtract, ALU.mult)
                last.then_inc(f_xn, 1)

            def ffn_low(f):
                n = f[0]
                dve.wait_ge(f_xh, n + 1)
                wait(dve, f_hmm, n * E * HC)
                V.tensor_tensor(xl[:, :], OUT[:, :], xh[:, :].bitcast(fp32), ALU.subtract).then_inc(f_split, 1)

            def ffn_logits(f):
                dve.wait_ge(f_logits, f[0] + 1)
                parts = H[0][:, 0:2 * TILES * E].rearrange("p (j k e) -> p j k e", k=2, e=E)
                V.tensor_copy(lg[:, :, :], parts[:, :, 0, :])
                dve.drain()
                V.tensor_tensor(lg[:, :, :], lg[:, :, :], parts[:, :, 1, :], ALU.add).then_inc(f_lread, 1)

            def ffn_top(f):
                dve.drain()
                for j in range(TILES):
                    V.max(m8[:, j, :], lg[:, j, :])
                dve.drain()
                V.tensor_tensor(gap[:, :], m8[:, :, 0], m8[:, :, 1], ALU.subtract).then_inc(f_gap, 1)
                for j in range(TILES):
                    V.max_index(ix[:, j, :], m8[:, j, :], lg[:, j, :])
                dve.drain()
                V.tensor_copy(ixf[:, :, :], ix[:, :, :])

            def ffn_weights(f):
                dve.wait_ge(f_th, f[0] + 1)
                V.tensor_scalar(c01[:, 0, :], th[:, :], 0.25, 0.25, ALU.mult, ALU.add)
                V.tensor_scalar(c01[:, 1, :], th[:, :], -0.25, 0.25, ALU.mult, ALU.add)
                dve.drain()
                iota = par("iota").unsqueeze(1).broadcast_to([P, TILES, E])
                for k in range(2):
                    V.tensor_tensor(hit[:, k, :, :], iota, ixf[:, :, k:k + 1].broadcast_to([P, TILES, E]),
                                    ALU.is_equal)
                dve.drain()
                for k in range(2):
                    V.tensor_tensor(hit[:, k, :, :], hit[:, k, :, :],
                                    c01[:, k, :].unsqueeze(2).broadcast_to([P, TILES, E]), ALU.mult)
                dve.drain()
                V.tensor_tensor(comb[:, :, :], hit[:, 0, :, :], hit[:, 1, :, :], ALU.add)
                dve.drain()

            def ffn_sum(f, e):
                n, src, dst, g, is_first = f
                dve.wait_ge(f_ymm, n * E + e + 1)
                wait(dve, f_yacc, n * E + e)
                if e == 0:
                    wait(dve, *((g_xam, g) if is_first else (s_store, g * 16)))
                for j in range(TILES):
                    last = V.scalar_tensor_tensor(
                        out=dst[:, j, :], in0=EOUT[e % 2][:, j * D:(j + 1) * D],
                        scalar=comb[:, j, e:e + 1], in1=(src if e == 0 else dst)[:, j, :],
                        op0=ALU.mult, op1=ALU.add)
                last.then_inc(f_yacc, 1)

            def mixer_norm_stats(g):
                dve.drain()
                norm_stats(xa, statm, mvm).then_inc(g_stats, 1)

            def mixer_norm(g):
                dve.wait_ge(g_rstd, g + 1)
                for j in range(TILES):
                    last = V.tensor_scalar(ln[:, j, :], xa[:, j, :], mvm[:, j, 0:1], rstdm[:, j:j + 1],
                                           ALU.subtract, ALU.mult)
                last.then_inc(g_ln, 1)

            def square_stats(src, tiles):
                norm_stats(src, statr, mvr, tiles)
                dve.drain()
                for j in tiles:
                    last = V.scalar_tensor_tensor(out=varr[:, j:j + 1], in0=mvr[:, j, 0:1], scalar=mvr[:, j, 0:1],
                                                  in1=mvr[:, j, 1:2], op0=ALU.mult, op1=ALU.add)
                last.then_inc(q_stats, 1)

            def square_norm(g, i, src, tiles):
                dve.wait_ge(q_rstd, turn_no(g, i) + 1)
                wait(dve, q_uTmm, turn_no(g, i))
                for j in tiles:
                    last = V.tensor_scalar(un[:, j, :], src[:, j, :], rstdr[:, j:j + 1], None, ALU.mult)
                last.then_inc(q_u, 1)

            def of_seq(b):
                return range(b * T // P, (b + 1) * T // P)

            def low_part(g, i):
                q, b = 4 * g + i, i % 2
                dve.wait_ge(q_bch, q + 1)
                lo = slice(2 * DS, 4 * DS)
                V.tensor_tensor(bcr[b][lo, :], W[0][lo, T:], bcr[b][lo, :].bitcast(fp32), ALU.subtract)\
                    .then_inc(q_bc, 1)

            def delta_u(g, i):
                q, b = 4 * g + i, i % 2
                dve.wait_ge(q_sp, q + 1)
                V.scalar_tensor_tensor(out=delta[b][:, :, :], in0=z[:, :, :], scalar=0.0, in1=ez[:, :, :],
                                       op0=ALU.max, op1=ALU.add).then_inc(q_delta, 1)
                dve.wait_ge(q_delta, q + 1)
                V.tensor_tensor(du[b][:, :, :], delta[b][:, :, :], xm[b][:, :, :], ALU.mult)
                dve.drain()

            def spread_rows(i, tile):
                return both(R[(SPREAD.index(tile) + SHIFT[i]) % RING]).unsqueeze(2).broadcast_to([P, DP, HALVES, T])

            def flat(b):
                return b[:, :, :, :].rearrange("p d h t -> p (d h t)")

            def scan_input(g, i, j):
                q = 4 * g + i
                dve.wait_ge(q_B, q * NP + j + 1)
                wait(dve, q_scan, q * NP + j - 1)
                V.tensor_tensor(dbu[j % 2][:, :, :, :],
                                du[i % 2][:, :, :].unsqueeze(1).broadcast_to([P, DP, HALVES, T]),
                                spread_rows(i, (0, j)), ALU.mult).then_inc(q_dbu, 1)

            def scan(g, i, j):
                q = 4 * g + i
                dve.wait_ge(q_dA, q * NP + j + 1)
                dve.wait_ge(q_dbu, q * NP + j + 1)
                wait(dve, q_G, q * NP + j - 1)
                V.tensor_tensor_scan(flat(hs[j % 2]), flat(dA[j % 4]), flat(dbu[j % 2]), 0.0, ALU.mult, ALU.add)\
                    .then_inc(q_scan, 1)

            def scan_output(g, i, j):
                q = 4 * g + i
                dve.wait_ge(q_C, q * NP + j + 1)
                dve.wait_ge(q_scan, q * NP + j + 1)
                last = j - NG if j >= NG else max(p for p in range(NP) if p % NG == j) - NP
                wait(dve, q_gs, q * (NP - 1) + (max(last, 1) if last >= 0 else last + 1))
                V.tensor_tensor(G[j % NG][:, :, :, :], hs[j % 2][:, :, :, :], spread_rows(i, (1, j)), ALU.mult)\
                    .then_inc(q_G, 1)

            def gate_y(g, i):
                q, b = 4 * g + i, i % 2
                dve.wait_ge(q_gs, (q + 1) * (NP - 1))
                dve.wait_ge(q_res, 2 * q + 2)
                wait(dve, q_omm, q)
                V.tensor_tensor(yg[:, :, :], acc[b][:, 0, :, :], acc[b][:, 1, :, :], ALU.add)
                dve.drain()
                for k in range(HALVES):
                    V.scalar_tensor_tensor(out=yg[:, k, :], in0=xm[b][:, k, :], scalar=par("D_ssm")[:, k:k + 1],
                                           in1=yg[:, k, :], op0=ALU.mult, op1=ALU.add)
                dve.drain()
                V.tensor_tensor(yg[:, :, :], yg[:, :, :], sres[b][:, :, :], ALU.mult).then_inc(q_yg, 1)

            def out_tiles(w):
                return w[:, 0:T].rearrange("p (j d) -> p j d", d=D)

            def first_sum(g, b):
                tiles = slice(b * T // P, (b + 1) * T // P)
                dve.wait_ge(q_omm, 4 * g + b + 1)
                wait(dve, g_rs, 2 * g + b - 1)
                V.tensor_tensor(x1[:, tiles, :], out_tiles(W[0]), ln[:, tiles, :], ALU.add).then_inc(g_x1, 1)
                dve.wait_ge(g_x1, 2 * g + b + 1)
                square_stats(x1, of_seq(b))

            def masked(g, b):
                dve.wait_ge(g_smm, 2 * g + b + 1)
                V.tensor_tensor(SM[:, :], W[1][:, 0:T + P], MT[:, :], ALU.mult).then_inc(g_sm, 1)

            def mixer_sum(g, b):
                tiles = slice(b * T // P, (b + 1) * T // P)
                dve.wait_ge(q_omm, 4 * g + 2 + b + 1)
                dve.wait_ge(g_rs, 2 * g + b + 1)
                V.tensor_tensor(xb[:, tiles, :], out_tiles(W[1]), rs[:, tiles, :], ALU.add).then_inc(g_xb, 1)

            def slot(g, i, tail, head, f, fx, nxt):
                ffn_steps = {"flog": ffn_logits, "ftop": ffn_top, "fweights": ffn_weights, "flow": ffn_low}
                next_steps = {"fstats": ffn_stats, "fnorm": ffn_norm}
                for name, num in steps("vector", i):
                    if name == "b":
                        scan_input(g, i, num)
                    elif name == "s":
                        scan(g, i, num)
                    elif name == "g":
                        scan_output(g, i, num)
                    elif name == "f":
                        if f:
                            ffn_sum(f, num)
                    elif name in ffn_steps:
                        if f:
                            ffn_steps[name](f)
                    elif name in next_steps:
                        if fx:
                            next_steps[name](fx)
                    elif name in ("lx", "ln", "unx"):
                        if nxt is not None:
                            if name == "lx":
                                mixer_norm_stats(nxt)
                            elif name == "ln":
                                mixer_norm(nxt)
                            else:
                                dve.wait_ge(g_ln, nxt + 1)
                                square_norm(nxt, 0, ln, range(TILES))
                    elif name in ("gate", "xsum", "mask", "xb"):
                        if tail and name == "gate":
                            gate_y(*tail)
                        elif tail:
                            {"xsum": first_sum, "mask": masked, "xb": mixer_sum}[name](tail[0], tail[1] % 2)
                    elif name == "un":
                        square_norm(*head, x1, of_seq(head[1] % 2))
                    elif head:
                        {"low": low_part, "delta": delta_u}[name](*head)

            def alone(f):
                ffn_stats(f)
                ffn_norm(f)
                ffn_low(f)
                ffn_logits(f)
                ffn_top(f)
                ffn_weights(f)
                for e in range(E):
                    ffn_sum(f, e)

            def start():
                f = (first(0), xin, xa, 0, True)
                split_gate()
                ffn_stats(f)
                exponent()
                ffn_norm(f)
                ffn_low(f)
                ffn_logits(f)
                split_w1()
                ffn_top(f)
                ffn_weights(f)
                mixer_weights()
                for e in range(E):
                    ffn_sum(f, e)
                f = (first(1), xin, xa, 1, True)
                mixer_norm_stats(0)
                ffn_stats(f)
                mixer_norm(0)
                ffn_norm(f)
                dve.wait_ge(g_ln, 1)
                square_norm(0, 0, ln, range(TILES))
                low_part(0, 0)
                delta_u(0, 0)

            def finish():
                gate_y(GROUPS - 1, 3)
                masked(GROUPS - 1, 1)
                mixer_sum(GROUPS - 1, 1)
                alone((second(GROUPS - 1), xb, ob, GROUPS - 1, False))

            def run(g, n1, n2, n3, is_last):
                f1 = n1 is not None and (n1, xin, xa, g + 1, True)
                f2 = n2 is not None and (n2, xb, ob, g - 1, False)
                f3 = n3 is not None and (n3, xin, xa, g + 2, True)
                for i in range(4):
                    tail = (g, i - 1) if i else None if isinstance(g, int) and g == 0 else (g - 1, 3)
                    head = (g, i + 1) if i < 3 else None if is_last else (g + 1, 0)
                    slot(g, i, tail, head, (f1, f2)[i // 2], (f2, f3)[i // 2], None if is_last else g + 1)

            start()
            run(0, first(1), None, first(2), False)
            with dve.Fori(1, GROUPS - 2) as g:
                run(g, g * 2, g * 2 + 1, g * 2 + 2, False)
            run(GROUPS - 2, first(GROUPS - 1), second(GROUPS - 3), None, False)
            run(GROUPS - 1, None, second(GROUPS - 2), None, True)
            finish()

        @block.gpsimd
        def _(pool):
            Q = nc.gpsimd
            Q.memset(powh[:, :], -0.5)
            Q.memset(epst[:, :], EPS)
            pool.drain()

            def root(v, r, tiles=slice(0, TILES)):
                Q.tensor_tensor(r[:, tiles], v, epst[:, tiles], ALU.add)
                pool.drain()
                return Q.tensor_tensor(r[:, tiles], r[:, tiles], powh[:, tiles], ALU.pow)

            def ffn_root(n):
                pool.wait_ge(f_stats, n + 1)
                root(mv[:, :, 1], rstd).then_inc(f_rstd, 1)

            def mixer_root(g):
                pool.wait_ge(g_stats, g + 1)
                root(mvm[:, :, 1], rstdm).then_inc(g_rstd, 1)
                Q.tensor_scalar(xam[:, :, :], xa[:, :, :], 1.0, 0.0, ALU.mult, ALU.add).then_inc(g_xam, 1)

            def entry_root(g):
                pool.wait_ge(g_rstd, g + 1)
                Q.tensor_tensor(vr[:, :], mvm[:, :, 1], rstdm[:, :], ALU.mult)
                pool.drain()
                Q.tensor_tensor(vr[:, :], vr[:, :], rstdm[:, :], ALU.mult)
                pool.drain()
                wait(pool, q_u, 3 * g)
                root(vr[:, :], rstdr).then_inc(q_rstd, 1)

            def mamba_root(g, i, tiles):
                pool.wait_ge(q_stats, 2 * g + i - 1)
                root(varr[:, tiles], rstdr, tiles).then_inc(q_rstd, 1)

            def pair_sum(g, i, j):
                q, b = 4 * g + i, i % 2
                pool.wait_ge(q_G, q * NP + j + 1)
                if j == 1:
                    wait(pool, q_yg, q - 1)
                else:
                    pool.wait_ge(q_gs, q * (NP - 1) + j - 1)
                Q.tensor_tensor(acc[b][:, :, :, :], (G[0] if j == 1 else acc[b])[:, :, :, :],
                                G[j % NG][:, :, :, :], ALU.add).then_inc(q_gs, 1)

            def residual(g, b):
                tiles = slice(b * T // P, (b + 1) * T // P)
                pool.wait_ge(g_x1, 2 * g + b + 1)
                wait(pool, g_xb, 2 * g + b - 1)
                Q.tensor_tensor(rs[:, tiles, :], xam[:, tiles, :], x1[:, tiles, :], ALU.add).then_inc(g_rs, 1)

            def slot(g, i, tail, head, n, nx, nxt):
                for name, num in steps("gpsimd", i):
                    if name == "a":
                        pair_sum(g, i, num)
                    elif name == "rms":
                        b = head[1] % 2
                        mamba_root(*head, slice(b * T // P, (b + 1) * T // P))
                    elif name == "rs":
                        residual(tail[0], tail[1])
                    elif name == "froot":
                        if nx is not None:
                            ffn_root(nx)
                    elif nxt is not None:
                        if name == "lnx":
                            mixer_root(nxt)
                        else:
                            entry_root(nxt)

            def start():
                ffn_root(first(0))
                mixer_root(0)
                ffn_root(first(1))
                entry_root(0)

            def finish():
                ffn_root(second(GROUPS - 1))

            def run(g, n1, n2, n3, is_last):
                for i in range(4):
                    tail = (g, i - 1) if i else None if isinstance(g, int) and g == 0 else (g - 1, 3)
                    head = (g, i + 1) if i < 3 else None if is_last else (g + 1, 0)
                    slot(g, i, tail, head, (n1, n2)[i // 2], (n2, n3)[i // 2], None if is_last else g + 1)

            start()
            run(0, first(1), None, first(2), False)
            with pool.Fori(1, GROUPS - 2) as g:
                run(g, g * 2, g * 2 + 1, g * 2 + 2, False)
            run(GROUPS - 2, first(GROUPS - 1), second(GROUPS - 3), None, False)
            run(GROUPS - 1, None, second(GROUPS - 2), None, True)
            finish()


def kernel(**inputs):
    import numpy as np
    import concourse.bacc as bacc
    from concourse.bass_utils import run_bass_kernel_spmd

    def a(name):
        return np.asarray(inputs["L0_" + name])

    def rows(m):
        return m.reshape(-1, P, m.shape[1]).transpose(1, 0, 2).reshape(P, -1)

    def fill(m, r=P):
        return np.concatenate([m, np.zeros((r - m.shape[0], m.shape[1]), m.dtype)], 0)

    t, s = np.arange(T)[None, :], np.arange(P)[:, None]
    xp = a("attn_x_proj_w")
    bc = np.concatenate([xp[DR:]] * 2, 0).T
    ob = a("attn_out_proj_b")
    f = np.float32
    taps = a("attn_conv_w")[:, 0, ::-1].T
    early = np.ascontiguousarray(np.concatenate(
        [a("attn_in_proj_w").T, np.broadcast_to(a("attn_in_proj_b")[None, :DI], (P, DI)),
         np.broadcast_to(taps.reshape(1, -1), (P, DC * DI))], 1))
    parts = {
        "gate": a("ffn_gate_w"),
        "xp_dt": rows(xp[:DR].T), "xp_bc": rows(bc), "out_w": rows(a("attn_out_proj_w").T),
        "write_w": a("attn_proj_write_w").T, "read_w": a("attn_proj_read_w").T,
        "norm1": a("attn_norm1_w")[:, None], "norm2": a("attn_norm2_w")[:, None],
        "in_b": rows(a("attn_in_proj_b")[:, None]), "conv_w": rows(a("attn_conv_w")[:, 0, :]),
        "conv_b": rows(a("attn_conv_b")[:, None]), "dt_b": rows(a("attn_dt_proj_b")[:, None]),
        "A_log": rows(a("attn_A_log")), "D_ssm": rows(a("attn_D_ssm")[:, None]), "out_b": ob[:, None],
        "decay": np.broadcast_to(a("attn_decay").reshape(1, 1), (P, 1)),
        "dt_w": fill(a("attn_dt_proj_w").T), "out_b_row": fill(ob[None, :]),
        "ident": np.eye(P, dtype=f), "dist": np.maximum(t - 1 - s, 0).astype(f), "causal": (t > s).astype(f),
        "iota": np.broadcast_to(np.arange(E, dtype=f), (P, E)),
        "tap_b": fill(taps), "ones_row": fill(np.ones((1, P), f)),
        "outside": fill(-(np.arange(PAD)[None, :] < np.arange(DC)[:, None]).astype(f)),
    }
    pack = np.ascontiguousarray(np.concatenate([parts[n] for n, _ in PACK], 1))
    sel = np.zeros((4 * DS, 2 * DS, P), f)
    sel[np.arange(4 * DS), np.arange(4 * DS) % (2 * DS), :] = 1.0
    arrays = {
        "x_dram": np.ascontiguousarray(a("attn_x").reshape(BATCH * T, D)), "pack_dram": pack,
        "early_dram": early,
        "sel_dram": sel.reshape(4 * DS, -1), "w1_dram": np.ascontiguousarray(a("ffn_w1s")),
        "w2_dram": np.ascontiguousarray(a("ffn_w2s")),
    }
    nc = bacc.Bacc("TRN2", target_bir_lowering=False, num_devices=1)
    args = [nc.dram_tensor(n, v.shape, mybir.dt.float32, kind="ExternalInput").ap() for n, v in arrays.items()]
    out = nc.dram_tensor("out_dram", (BATCH * T, D), mybir.dt.float32, kind="ExternalOutput").ap()
    moe_mamba_kernel(nc, *args, out)
    r = run_bass_kernel_spmd(nc, [arrays], core_ids=[0])
    return r.results[0]["out_dram"].reshape(BATCH, T, D)
```
